# Optimizing a Trainium2 kernel written in Bass

```python
import numpy as np
import jax
import jax.numpy as jnp

def _softmax(x, axis=-1):
    return jax.nn.softmax(x, axis=axis)
def _gelu(x):
    return jax.nn.gelu(x, approximate=True)
def _silu(x):
    return jax.nn.silu(x)
def _sigmoid(x):
    return jax.nn.sigmoid(x)
def _layernorm(x, axis=-1, eps=1e-5):
    m = jnp.mean(x, axis=axis, keepdims=True)
    v = jnp.var(x, axis=axis, keepdims=True)
    return (x - m) / jnp.sqrt(v + eps)
def _scatter_add(tgt, idx, src, axis=0):
    return tgt.at[idx].add(src)
def _segment_sum(src, seg, n):
    return jax.ops.segment_sum(src, seg, n)

kernel_name = 'mk_adj_preln_d2_adj_256_a7e1ba'

def setup_inputs(seed: int = 0):
    np.random.seed(seed)
    _w = jnp.asarray
    def _rec_inputs():
        import jax
        import jax.numpy as jnp
        _gk = jax.random.key(seed)
        x = -0.0005207 + 1.001 * jax.random.normal(jax.random.fold_in(_gk, 1), (8, 2048, 256), jnp.float32)
        _w = (1.0 + jnp.arange(2048, dtype=jnp.float32)) ** -0.5
        _w = _w / _w.mean()
        _pij = jnp.clip(0.00390625 * _w[:, None] * _w[None, :], 0.0, 1.0)
        _a = jax.random.uniform(jax.random.fold_in(_gk, 2), (2048, 2048)) < _pij
        adj = _a.astype(jnp.int32)
        return x, adj
    x, adj = _rec_inputs()
    def _L0_gnn_setup():
        import jax, jax.numpy as jnp
        import numpy as np
        import math
        CHUNK = 256
        NUM_HEADS = 4
        EPS = 1e-05
        key = jax.random.key(seed)
        ks = jax.random.split(key, 12)
        B, N, F = (4, 2048, 256)
        x = jax.random.normal(ks[0], (B, N, F), dtype=jnp.float32)
        adj_matrix = jax.random.randint(ks[1], (N, N), 0, 2, dtype=jnp.int32)
        s = 1.0 / math.sqrt(F)
        Wq = jax.random.normal(ks[2], (F, F), dtype=jnp.float32) * s
        bq = jnp.zeros((F,), dtype=jnp.float32)
        Wk = jax.random.normal(ks[3], (F, F), dtype=jnp.float32) * s
        bk = jnp.zeros((F,), dtype=jnp.float32)
        Wv = jax.random.normal(ks[4], (F, F), dtype=jnp.float32) * s
        bv = jnp.zeros((F,), dtype=jnp.float32)
        Wo = jax.random.normal(ks[5], (F, F), dtype=jnp.float32) * s
        bo = jnp.zeros((F,), dtype=jnp.float32)
        gamma = jnp.ones((F,), dtype=jnp.float32)
        beta = jnp.zeros((F,), dtype=jnp.float32)
        return {'x': x, 'adj_matrix': adj_matrix, 'Wq': Wq, 'bq': bq, 'Wk': Wk, 'bk': bk, 'Wv': Wv, 'bv': bv, 'Wo': Wo, 'bo': bo, 'gamma': gamma, 'beta': beta}
    _L0_gnn_all = _L0_gnn_setup()
    _L0_gnn_in = {k: v for k, v in _L0_gnn_all.items() if k in ('Wq', 'bq', 'Wk', 'bk', 'Wv', 'bv', 'Wo', 'bo', 'gamma', 'beta', )}
    del _L0_gnn_all

    def _L1_gnn_setup():
        import jax, jax.numpy as jnp
        import numpy as np
        IN_DIM = 256
        OUT_DIM = 64
        NUM_HEADS = 4
        ALPHA = 0.2
        NEG_INF = -9000000000000000.0
        key = jax.random.key(seed)
        k1, k2, k3, k4 = jax.random.split(key, 4)
        B, N = (4, 2048)
        h = jax.random.normal(k1, (B, N, IN_DIM), dtype=jnp.float32)
        adj = jax.random.randint(k2, (N, N), 0, 2, dtype=jnp.int32)
        W = jax.random.normal(k3, (IN_DIM, NUM_HEADS * OUT_DIM), dtype=jnp.float32) * (1.0 / np.sqrt(IN_DIM))
        a = jax.random.normal(k4, (2 * OUT_DIM,), dtype=jnp.float32) * (1.0 / np.sqrt(2 * OUT_DIM))
        return {'h': h, 'adj': adj, 'W': W, 'a': a}
    _L1_gnn_all = _L1_gnn_setup()
    _L1_gnn_in = {k: v for k, v in _L1_gnn_all.items() if k in ('W', 'a', )}
    del _L1_gnn_all

    return {
        "x": x,
        "adj": adj,
        "L0_gnn_Wq": _L0_gnn_in["Wq"],
        "L0_gnn_bq": _L0_gnn_in["bq"],
        "L0_gnn_Wk": _L0_gnn_in["Wk"],
        "L0_gnn_bk": _L0_gnn_in["bk"],
        "L0_gnn_Wv": _L0_gnn_in["Wv"],
        "L0_gnn_bv": _L0_gnn_in["bv"],
        "L0_gnn_Wo": _L0_gnn_in["Wo"],
        "L0_gnn_bo": _L0_gnn_in["bo"],
        "L0_gnn_gamma": _L0_gnn_in["gamma"],
        "L0_gnn_beta": _L0_gnn_in["beta"],
        "L1_gnn_W": _L1_gnn_in["W"],
        "L1_gnn_a": _L1_gnn_in["a"],
    }

def reference(x, adj, L0_gnn_Wq, L0_gnn_bq, L0_gnn_Wk, L0_gnn_bk, L0_gnn_Wv, L0_gnn_bv, L0_gnn_Wo, L0_gnn_bo, L0_gnn_gamma, L0_gnn_beta, L1_gnn_W, L1_gnn_a):
    import jax
    import jax.numpy as jnp
    def _L0_gnn_ref(x, adj_matrix, Wq, bq, Wk, bk, Wv, bv, Wo, bo, gamma, beta):
        import jax, jax.numpy as jnp
        import numpy as np
        import math
        CHUNK = 256
        NUM_HEADS = 4
        EPS = 1e-05
        B, N, Fin = x.shape
        H = NUM_HEADS
        Dout = Wq.shape[0]
        Dh = Dout // H
        Nc = N // CHUNK
        q = (x @ Wq.T + bq).reshape(B, N, H, Dh).transpose(0, 2, 1, 3)
        k = (x @ Wk.T + bk).reshape(B, N, H, Dh).transpose(0, 2, 1, 3)
        v = (x @ Wv.T + bv).reshape(B, N, H, Dh).transpose(0, 2, 1, 3)
        kc = k.reshape(B, H, Nc, CHUNK, Dh)
        vc = v.reshape(B, H, Nc, CHUNK, Dh)
        scores = jnp.einsum('bhnd,bhjcd->bhnjc', q, kc) / jnp.sqrt(jnp.asarray(Dh, dtype=q.dtype))
        scores = jnp.clip(scores, -10.0, 10.0)
        mask = adj_matrix.reshape(N, Nc, CHUNK)[None, None]
        scores = jnp.where(mask == 0, jnp.asarray(-10.0, scores.dtype), scores)
        attn = jax.nn.softmax(scores, axis=-1)
        ctx = jnp.einsum('bhnjc,bhjcd->bhnd', attn, vc)
        ctx = ctx.transpose(0, 2, 1, 3).reshape(B, N, Dout)
        out = ctx @ Wo.T + bo
        out = out + x
        mu = jnp.mean(out, axis=-1, keepdims=True)
        var = jnp.mean(jnp.square(out - mu), axis=-1, keepdims=True)
        out = (out - mu) * jax.lax.rsqrt(var + EPS) * gamma + beta
        return out

    def _L1_gnn_ref(h, adj, W, a):
        import jax, jax.numpy as jnp
        import numpy as np
        IN_DIM = 256
        OUT_DIM = 64
        NUM_HEADS = 4
        ALPHA = 0.2
        NEG_INF = -9000000000000000.0
        B, N, _ = h.shape
        H, D = (NUM_HEADS, OUT_DIM)
        q = (h @ W).reshape(B, N, H, D)
        a_src, a_dst = (a[:D], a[D:])
        e_src = jnp.einsum('bnhd,d->bnh', q, a_src)
        e_dst = jnp.einsum('bnhd,d->bnh', q, a_dst)
        e = e_src[:, :, None, :] + e_dst[:, None, :, :]
        e = jnp.where(e >= 0, e, ALPHA * e)
        mask = (adj > 0)[None, :, :, None]
        e = jnp.where(mask, e, NEG_INF)
        attn = jax.nn.softmax(e, axis=2)
        h_prime = jnp.einsum('bijh,bjhd->bihd', attn, q)
        return jax.nn.elu(h_prime.reshape(B, N, H * D))

    h = jnp.maximum(_layernorm(x, axis=-1), 0.0)
    x = x + _L0_gnn_ref(h, adj, L0_gnn_Wq, L0_gnn_bq, L0_gnn_Wk, L0_gnn_bk, L0_gnn_Wv, L0_gnn_bv, L0_gnn_Wo, L0_gnn_bo, L0_gnn_gamma, L0_gnn_beta)
    h = jnp.maximum(_layernorm(x, axis=-1), 0.0)
    x = x + _L1_gnn_ref(h, adj, L1_gnn_W, L1_gnn_a)
    return x


_drawn_inputs = setup_inputs


def setup_inputs(seed=0):
    import zlib

    import numpy as np

    out = dict(_drawn_inputs(seed))
    spreads = {'L0_gnn_bq': (0.0, 0.8),
     'L0_gnn_bk': (0.0, 0.8),
     'L0_gnn_bv': (0.0, 0.1),
     'L0_gnn_bo': (0.0, 0.411),
     'L0_gnn_gamma': (1.0, 0.2),
     'L0_gnn_beta': (0.0, 0.1)}
    factors = {}
    for name, (base, spread) in spreads.items():
        noise = np.random.default_rng([zlib.crc32(name.encode()), seed]).standard_normal(out[name].shape)
        drawn = base * np.exp(spread * noise) if base else spread * noise
        out[name] = jnp.asarray(drawn.astype(out[name].dtype))
    for name, factor in factors.items():
        out[name] = (out[name] * factor).astype(out[name].dtype)
    return out
```

```python
import math

import concourse.bass as bass
from concourse import mybir
from contextlib import ExitStack

ALU = mybir.AluOpType
ACT = mybir.ActivationFunctionType
AX_X = mybir.AxisListType.X
F32 = mybir.dt.float32
F16 = mybir.dt.float16
I32 = mybir.dt.int32
U8 = mybir.dt.uint8
RMAX = bass.bass_isa.ReduceOp.max

P = 128
IW = 512
CHUNK = 256
CLIP = 10.0
EPS = 1e-5
ALPHA = 0.2
LAG = 2
EBUF = 4


def spread(ap, n):
    p, m = ap.shape
    return ap.rearrange("p (a m) -> p a m", a=1).broadcast_to([p, n, m])


def layer0(nc, x, adjT, wqT, bq, wkT, bk, wvT, bv, woT, bo, gamma, beta, x1):
    B, N, F = x.shape
    NT = N // P
    KT = F // P
    D = F // 4
    PAIRS = F // (2 * D)
    IB = N // IW
    NCH = N // CHUNK
    JC = CHUNK // P
    assert PAIRS == KT == 2 and 2 * D == P and JC == 2 and NT % EBUF == 0
    LO, HI = math.exp(-CLIP), math.exp(CLIP)

    G_TR, G_V, G_QK, G_WO = KT * NT // 4, NT // 2, 2 * IB, NT // 2
    G_B = G_TR + G_V + PAIRS * G_QK + G_WO
    T_IB, T_PR, T_B = NT, IB * NT, PAIRS * IB * NT
    C_IB, C_PR, C_B = NCH, IB * NCH, PAIRS * IB * NCH
    S_PR = 12 * 16

    with ExitStack() as ctx_:
        def sb(name, shape, dt):
            return ctx_.enter_context(nc.sbuf_tensor(name, shape, dt))

        def sem(name):
            return ctx_.enter_context(nc.semaphore(name))

        mask = sb("a_mask", [P, NT, N], U8)
        xin = sb("a_x", [P, NT, F], F32)
        h = sb("a_h", [P, NT, F], F32)
        hT = sb("a_hT", [P, KT, N], F32)
        v = sb("a_v", [P, NT, F], F32)
        ctxT = sb("a_ctxT", [P, PAIRS, N], F32)
        q_st = sb("a_q_st", [P, 2, N], F16)
        kh_st = sb("a_kh_st", [P, 2, N], F16)
        kl_st = sb("a_kl_st", [P, 2, N], F16)
        q_hi, q_lo = sb("a_q_hi", [P, N], F16), sb("a_q_lo", [P, N], F16)
        k_hi, k_lo = sb("a_k_hi", [P, N], F16), sb("a_k_lo", [P, N], F16)
        e = sb("a_e", [P, EBUF, 2, IW], F32)
        wq, wk = sb("a_wq", [P, KT, F], F32), sb("a_wk", [P, KT, F], F32)
        wv, wo = sb("a_wv", [P, KT, F], F32), sb("a_wo", [P, KT, F], F32)
        bq_c, bk_c = sb("a_bq", [P, PAIRS], F32), sb("a_bk", [P, PAIRS], F32)
        bv_r, bo_r = sb("a_bv", [P, F], F32), sb("a_bo", [P, F], F32)
        gamma_r, beta_r = sb("a_gamma", [P, F], F32), sb("a_beta", [P, F], F32)
        rz = sb("a_rz", [P, 2, IW], F32)
        scaled = sb("a_scaled", [P, 2, IW], F32)
        ident = sb("a_ident", [P, P], F32)
        ones = sb("a_ones", [P, D], F32)
        stats = sb("a_stats", [P, NT, 6], F32)
        mv = sb("a_mv", [P, NT, 2], F32)
        var_eps = sb("a_var", [P, NT], F32)
        half_neg = sb("a_half", [P, NT], F32)
        rstd = sb("a_rstd", [P, NT], F32)
        shift = sb("a_shift", [P, NT], F32)
        sc = ctx_.enter_context(nc.psum_tensor("a_sc", [P, 4, IW], F32))
        num = ctx_.enter_context(nc.psum_tensor("a_num", [P, 2, IW], F32))
        den = ctx_.enter_context(nc.psum_tensor("a_den", [P, 2, IW], F32))

        weights_in = sem("a_weights_in")
        adj_in = [sem("a_adj_in0"), sem("a_adj_in1")]
        mask_built = sem("a_mask_built")
        const_ready = sem("a_const_ready")
        x_in = sem("a_x_in")
        x_free = sem("a_x_free")
        x1_stored = sem("a_x1_stored")
        waited = sem("a_waited")
        stats_made = sem("a_stats_made")
        mv_ready = sem("a_mv_ready")
        pool_step = sem("a_pool_step")
        rstd_ready = sem("a_rstd_ready")
        shift_ready = sem("a_shift_ready")
        h_ready = sem("a_h_ready")
        group_ready = sem("a_group_ready")
        group_free = sem("a_group_free")
        hi_ready = sem("a_hi_ready")
        stacked = sem("a_stacked")
        bias_added = sem("a_bias_added")
        scores_ready = sem("a_scores_ready")
        exp_ready = sem("a_exp_ready")
        masked = sem("a_masked")
        p_ready = sem("a_p_ready")
        p_used = sem("a_p_used")
        ln_ready = sem("a_ln_ready")
        rz_ready = sem("a_rz_ready")
        chunk_free = sem("a_chunk_free")
        ctx_done = sem("a_ctx_done")
        post_step = sem("a_post_step")
        out_ready = sem("a_out_ready")

        block = ctx_.enter_context(nc.Block())

        def stage(t):
            return e[:, 2 * (t % 2):2 * (t % 2) + 2, :, :].rearrange("p a b n -> p (a b n)").bitcast(I32)

        @block.sync
        def _(sp):
            for w, src in ((wq, wqT), (wk, wkT), (wv, wvT), (wo, woT)):
                sp.dma_start(w[:], src.rearrange("(k p) n -> p k n", p=P)).then_inc(weights_in, 16)
            for c, src in ((bq_c, bq), (bk_c, bk)):
                sp.dma_start(c[:], src).then_inc(weights_in, 16)
            for r, src in ((bv_r, bv), (bo_r, bo), (gamma_r, gamma), (beta_r, beta)):
                sp.dma_start(r[:], src.rearrange("(a n) -> a n", a=1).broadcast_to([P, F])).then_inc(weights_in, 16)
            for t in range(NT):
                if t >= 2:
                    sp.wait_ge(mask_built, t - 1)
                sp.dma_start(stage(t), adjT[t * P:(t + 1) * P, :]).then_inc(adj_in[t % 2], 16)
            sp.sem_inc(x1_stored, 16)
            with sp.Fori(0, B) as b:
                sp.wait_ge(x_free, b + 1)
                sp.dma_start(xin[:], x[bass.ds(b, 1), :, :].rearrange("a (t p) f -> p (a t) f", p=P)).then_inc(x_in, 16)
                for pr in range(PAIRS):
                    sp.wait_ge(group_free, b * G_B + 4 + G_TR + G_V + (pr + 1) * G_QK)
                    for hd in range(2):
                        mine = slice(hd * D, (hd + 1) * D)
                        for dst, top, low in ((q_st, q_hi, q_lo), (kh_st, k_hi, k_hi), (kl_st, k_lo, k_lo)):
                            sp.dma_start(dst[0:D, hd, :], top[mine, :]).then_inc(stacked, 16)
                            sp.dma_start(dst[D:P, hd, :], low[mine, :]).then_inc(stacked, 16)
                sp.wait_ge(out_ready, b + 1)
                sp.dma_start(x1[bass.ds(b, 1), :, :].rearrange("a (t p) f -> p (a t) f", p=P), h[:]).then_inc(x1_stored, 16)
            sp.wait_ge(x1_stored, 16 * (B + 1))

        @block.gpsimd
        def _(pool):
            pool.memset(ident[:], 0.0).then_inc(pool_step, 1)
            pool.memset(ones[:], 1.0).then_inc(const_ready, 1)
            pool.memset(half_neg[:], -0.5).then_inc(pool_step, 1)
            pool.wait_ge(pool_step, 2)
            pool.affine_select(out=ident[:], in_=ident[:], compare_op=ALU.not_equal, fill=1.0, base=0,
                               pattern=[[-1, P]], channel_multiplier=1).then_inc(const_ready, 1)
            pool.wait_ge(weights_in, 160)

            def make_rstd(b, k):
                pool.wait_ge(mv_ready, 2 * b + k + 1)
                pool.sem_inc(waited, 1)
                nc.gpsimd.tensor_scalar(var_eps[:], mv[:, :, 1], EPS, None, ALU.add).then_inc(pool_step, 1)
                pool.wait_ge(pool_step, 2 * b + k + 3)
                nc.gpsimd.tensor_tensor(rstd[:], var_eps[:], half_neg[:], ALU.pow).then_inc(rstd_ready, 1)

            with pool.Fori(0, B) as b:
                make_rstd(b, 0)
                pool.wait_ge(group_ready, b * G_B + G_TR)
                nc.gpsimd.tensor_tensor(h[:], h[:], spread(bo_r[:], NT), ALU.add).then_inc(bias_added, 1)
                nc.gpsimd.tensor_tensor(xin[:], xin[:], spread(beta_r[:], NT), ALU.add).then_inc(bias_added, 1)
                make_rstd(b, 1)

        @block.scalar
        def _(act):
            nc.scalar.preload_act_table_set("natural_log_exp_and_others")
            act.wait_ge(weights_in, 160)
            act.wait_ge(mask_built, NT)

            def invert(done, c):
                act.wait_ge(p_used, EBUF + JC * (done + 1))
                nc.scalar.activation(rz[:, c, :], den[:, c, :], ACT.Ln).then_inc(ln_ready, 1)
                act.wait_ge(ln_ready, done + 1)
                nc.scalar.activation(rz[:, c, :], rz[:, c, :], ACT.Exp, scale=-1.0).then_inc(rz_ready, 1)

            with act.Fori(0, B) as b:
                act.wait_ge(shift_ready, b + 1)
                act.wait_ge(x1_stored, 16 * b + 16)
                for t in range(NT):
                    nc.scalar.activation(h[:, t, :], xin[:, t, :], ACT.Relu, bias=shift[:, t:t + 1],
                                         scale=rstd[:, t:t + 1]).then_inc(h_ready, 1)
                for pr in range(PAIRS):
                    for g in range(G_QK):
                        to, bias = ((q_hi, bq_c), (k_hi, bk_c))[g // IB]
                        act.wait_ge(group_ready, b * G_B + G_TR + G_V + pr * G_QK + g + 1)
                        nc.scalar.activation(to[:, (g % IB) * IW:(g % IB + 1) * IW], sc[:, g % 4, :], ACT.Identity,
                                             bias=bias[:, pr:pr + 1]).then_inc(hi_ready, 1)
                    t0, c0 = b * T_B + pr * T_PR, b * C_B + pr * C_PR

                    def block_of(ib, first):
                        for jt in range(NT):
                            at = t0 + ib * T_IB + jt
                            act.wait_ge(scores_ready, at + 1)
                            act.wait_ge(p_used, at + 1)
                            nc.scalar.activation(e[:, jt % EBUF, :, :], sc[:, 2 * (jt % 2):2 * (jt % 2) + 2, :],
                                                 ACT.Exp, scale=float(D) ** -0.5).then_inc(exp_ready, 1)
                            if jt % JC == 0 and not (first and jt < LAG * JC):
                                invert(c0 + ib * C_IB + jt // JC - LAG, (jt // JC) % 2)

                    block_of(0, True)
                    with act.Fori(1, IB) as ib:
                        block_of(ib, False)
                    for c in range(LAG):
                        invert(c0 + C_PR - LAG + c, c % 2)

        @block.vector
        def _(dve):
            for t in range(NT):
                dve.wait_ge(adj_in[t % 2], 16 * (t // 2 + 1))
                nc.vector.tensor_scalar(mask[:, t, :], stage(t), 0.0, None, ALU.not_equal).then_inc(mask_built, 1)
            dve.sem_inc(x_free, 1)
            dve.sem_inc(group_free, 4)
            dve.sem_inc(chunk_free, 2)
            dve.wait_ge(weights_in, 160)

            def layer_norm_stats(b, k, src):
                for t in range(NT):
                    nc.vector.bn_stats(stats[:, t, :], src[:, t, :]).then_inc(stats_made, 1)
                dve.wait_ge(stats_made, (2 * b + k + 1) * NT)
                dve.sem_inc(waited, 1)
                for t in range(NT):
                    last = nc.vector.bn_aggr(mv[:, t, :], stats[:, t, :])
                last.then_inc(mv_ready, 1)

            def weigh(at, ib, jt):
                slot = e[:, jt % EBUF, :, :]
                dve.wait_ge(exp_ready, at + 1)
                nc.vector.scalar_tensor_tensor(slot, slot, HI, spread(mask[:, jt, bass.ds(ib * IW, IW)], 2),
                                               ALU.min, ALU.mult).then_inc(masked, 1)
                dve.wait_ge(masked, at + 1)
                nc.vector.tensor_scalar(slot, slot, LO, None, ALU.max).then_inc(p_ready, 1)

            def normalise(done, c, cols, fresh):
                dve.wait_ge(rz_ready, done + 1)
                if fresh:
                    nc.vector.tensor_tensor(cols, num[:, c, :], rz[:, c, :], ALU.mult).then_inc(chunk_free, 1)
                else:
                    nc.vector.tensor_tensor(scaled[:, c, :], num[:, c, :], rz[:, c, :], ALU.mult).then_inc(chunk_free, 1)
                    dve.wait_ge(chunk_free, done + 3)
                    nc.vector.tensor_tensor(cols, cols, scaled[:, c, :], ALU.add)

            with dve.Fori(0, B) as b:
                dve.wait_ge(x_in, 16 * b + 16)
                layer_norm_stats(b, 0, xin)
                dve.wait_ge(rstd_ready, 2 * b + 1)
                nc.vector.scalar_tensor_tensor(shift[:], mv[:, :, 0], -1.0, rstd[:], ALU.mult,
                                               ALU.mult).then_inc(shift_ready, 1)
                for g in range(G_TR):
                    dve.wait_ge(group_ready, b * G_B + g + 1)
                    nc.vector.tensor_copy(hT[:, g % KT, (g // KT) * IW:(g // KT + 1) * IW],
                                          sc[:, g % 4, :]).then_inc(group_free, 1)
                for g in range(G_V):
                    dve.wait_ge(group_ready, b * G_B + G_TR + g + 1)
                    nc.vector.tensor_tensor(v[:, 2 * g:2 * g + 2, :],
                                            sc[:, g % 4, :].rearrange("p (a f) -> p a f", a=2),
                                            spread(bv_r[:], 2), ALU.add).then_inc(group_free, 1)
                for pr in range(PAIRS):
                    for g in range(G_QK):
                        hi, lo, bias = ((q_hi, q_lo, bq_c), (k_hi, k_lo, bk_c))[g // IB]
                        cols = slice((g % IB) * IW, (g % IB + 1) * IW)
                        dve.wait_ge(hi_ready, (b * PAIRS + pr) * G_QK + g + 1)
                        nc.vector.scalar_tensor_tensor(lo[:, cols], sc[:, g % 4, :], bias[:, pr:pr + 1],
                                                       hi[:, cols], ALU.add, ALU.subtract).then_inc(group_free, 1)
                    t0, c0 = b * T_B + pr * T_PR, b * C_B + pr * C_PR

                    def block_of(ib, first):
                        for jt in range(NT):
                            weigh(t0 + ib * T_IB + jt, ib, jt)
                            if jt % JC == 0 and not (first and jt < LAG * JC):
                                c = jt // JC - LAG
                                cols = ctxT[:, pr, bass.ds((ib if c >= 0 else ib - 1) * IW, IW)]
                                normalise(c0 + ib * C_IB + c, c % 2, cols, c == 0)

                    block_of(0, True)
                    with dve.Fori(1, IB) as ib:
                        block_of(ib, False)
                    for c in range(NCH - LAG, NCH):
                        normalise(c0 + C_PR - NCH + c, c % 2, ctxT[:, pr, N - IW:N], False)
                dve.drain().then_inc(ctx_done, 1)
                dve.wait_ge(bias_added, 2 * b + 2)
                for g in range(G_WO):
                    dve.wait_ge(group_ready, b * G_B + G_B - G_WO + g + 1)
                    rows = h[:, 2 * g:2 * g + 2, :]
                    nc.vector.tensor_tensor(rows, sc[:, g % 4, :].rearrange("p (a f) -> p a f", a=2), rows,
                                            ALU.add).then_inc(group_free, 1)
                dve.wait_ge(group_free, b * G_B + 4 + G_B)
                layer_norm_stats(b, 1, h)
                dve.wait_ge(rstd_ready, 2 * b + 2)
                for t in range(NT):
                    nc.vector.scalar_tensor_tensor(h[:, t, :], h[:, t, :], mv[:, t, 0:1], gamma_r[:], ALU.subtract,
                                                   ALU.mult).then_inc(post_step, 1)
                for t in range(NT):
                    dve.wait_ge(post_step, b * NT + t + 1)
                    last = nc.vector.scalar_tensor_tensor(h[:, t, :], h[:, t, :], rstd[:, t:t + 1], xin[:, t, :],
                                                          ALU.mult, ALU.add)
                last.then_inc(out_ready, 1)
                dve.wait_ge(out_ready, b + 1)
                dve.sem_inc(x_free, 1)

        @block.tensor
        def _(pe):
            pe.wait_ge(const_ready, 2)
            pe.wait_ge(weights_in, 160)
            pe.sem_inc(p_used, EBUF)

            def group(b, g):
                pe.wait_ge(group_free, b * G_B + g + 1)

            def score(ib, jt):
                rows = slice(jt * P, (jt + 1) * P)
                for hd in range(2):
                    out = sc[:, 2 * (jt % 2) + hd, :]
                    q = q_st[:, hd, bass.ds(ib * IW, IW)]
                    nc.tensor.matmul(out, kh_st[:, hd, rows], q, start=True, stop=False)
                    last = nc.tensor.matmul(out, kl_st[:, hd, rows], q, start=False, stop=True)
                last.then_inc(scores_ready, 1)

            def apply(at, done, jt, pr):
                c = (jt // JC) % 2
                if jt % JC == 0:
                    pe.wait_ge(chunk_free, done + 1)
                pe.wait_ge(p_ready, at + 1)
                first, final = jt % JC == 0, jt % JC == JC - 1
                for hd in range(2):
                    nc.tensor.matmul(num[hd * D:(hd + 1) * D, c, :],
                                     v[:, jt, pr * P + hd * D:pr * P + (hd + 1) * D],
                                     e[:, jt % EBUF, hd, :], start=first, stop=final)
                for hd in range(2):
                    last = nc.tensor.matmul(den[hd * D:(hd + 1) * D, c, :], ones[:],
                                            e[:, jt % EBUF, hd, :], start=first, stop=final)
                last.then_inc(p_used, 1)

            with pe.Fori(0, B) as b:
                for g in range(G_TR):
                    group(b, g)
                    pe.wait_ge(h_ready, b * NT + 4 * (g // KT) + 4)
                    for k in range(4):
                        t = 4 * (g // KT) + k
                        last = nc.tensor.transpose(sc[:, g % 4, k * P:(k + 1) * P],
                                                   h[:, t, (g % KT) * P:(g % KT + 1) * P], ident[:])
                    last.then_inc(group_ready, 1)
                pe.wait_ge(group_free, b * G_B + 4 + G_TR)
                for g in range(G_V):
                    group(b, G_TR + g)
                    for k in range(2):
                        t = 2 * g + k
                        for kt in range(KT):
                            last = nc.tensor.matmul(sc[:, g % 4, k * F:(k + 1) * F], hT[:, kt, t * P:(t + 1) * P],
                                                    wv[:, kt, :], start=(kt == 0), stop=(kt == KT - 1))
                    last.then_inc(group_ready, 1)
                for pr in range(PAIRS):
                    t0, c0 = b * T_B + pr * T_PR, b * C_B + pr * C_PR
                    if pr:
                        pe.wait_ge(exp_ready, t0)
                    for g in range(G_QK):
                        group(b, G_TR + G_V + pr * G_QK + g)
                        w = (wq, wk)[g // IB]
                        for kt in range(KT):
                            last = nc.tensor.matmul(sc[:, g % 4, :], w[:, kt, pr * P:(pr + 1) * P],
                                                    hT[:, kt, (g % IB) * IW:(g % IB + 1) * IW],
                                                    start=(kt == 0), stop=(kt == KT - 1))
                        last.then_inc(group_ready, 1)
                    pe.wait_ge(group_free, b * G_B + 4 + G_TR + G_V + (pr + 1) * G_QK)
                    pe.wait_ge(stacked, (b * PAIRS + pr + 1) * S_PR)
                    score(0, 0)
                    score(0, 1)

                    def block_of(ib, last):
                        for jt in range(NT):
                            at = t0 + ib * T_IB + jt
                            if jt + 2 < NT or not last:
                                pe.wait_ge(exp_ready, at + 1)
                                score(ib + (jt + 2) // NT, (jt + 2) % NT)
                            apply(at, c0 + ib * C_IB + jt // JC, jt, pr)

                    with pe.Fori(0, IB - 1) as ib:
                        block_of(ib, False)
                    block_of(IB - 1, True)
                pe.wait_ge(exp_ready, (b + 1) * T_B)
                pe.wait_ge(ctx_done, b + 1)
                for g in range(G_WO):
                    group(b, G_B - G_WO + g)
                    for k in range(2):
                        t = 2 * g + k
                        for pr in range(PAIRS):
                            last = nc.tensor.matmul(sc[:, g % 4, k * F:(k + 1) * F], ctxT[:, pr, t * P:(t + 1) * P],
                                                    wo[:, pr, :], start=(pr == 0), stop=(pr == PAIRS - 1))
                    last.then_inc(group_ready, 1)


def layer1(nc, x1, adjT, w, a, s_rows_dram, out):
    B, N, F = x1.shape
    NT, KT, D = N // P, F // P, F // 4
    HEADS = F // D
    HW = 2 * IW
    HALVES = N // HW
    FX = F + 2 * HEADS
    NH = KT * HALVES
    PB = 4
    TK = IW // P
    G_TR, G_PJ = KT * NT // 4, NT
    G_PREP = G_TR + G_PJ + 2
    G_END = 1 + HALVES
    assert HALVES == 2 and KT == 2 and G_PREP % 2 == 0 and (NH * G_END) % 2 == 0

    with ExitStack() as ctx_:
        def sb(name, shape, dt):
            return ctx_.enter_context(nc.sbuf_tensor(name, shape, dt))

        def sem(name):
            return ctx_.enter_context(nc.semaphore(name))

        mask = sb("b_mask", [P, NT, N], U8)
        xin = sb("b_x", [P, NT, F], F32)
        h = sb("b_h", [P, NT, F], F32)
        hT = sb("b_hT", [P, KT, N], F32)
        v = sb("b_v", [P, NT, FX], F32)
        g32 = sb("b_g32", [P, NT, HEADS, 32], F32)
        r = sb("b_r", [P, HEADS, N], F32)
        p = sb("b_p", [P, PB, 2, HW], F32)
        num_s = sb("b_num_s", [P, 2, 2, IW], F32)
        den_s = sb("b_den_s", [P, 2, IW], F32)
        y = sb("b_y", [P, 2 * TK, P], F32)
        neg = sb("b_neg", [P, 2 * TK, P], F32)
        wx = sb("b_wx", [P, KT, FX], F32)
        a_r = sb("b_a", [P, 2 * D], F32)
        wa = sb("b_wa", [P, HEADS, D], F32)
        ident = sb("b_ident", [P, P], F32)
        ones = sb("b_ones", [P, 32], F32)
        ones_h = sb("b_ones_h", [P, 1], F16)
        lone = sb("b_lone", [1, N], F32)
        mean_v = sb("b_mean_v", [1, F], F32)
        s_c = sb("b_s_c", [P, HEADS, NT], F32)
        s_rows = sb("b_s_rows", [HEADS * NT, P], F32)
        g = sb("b_g", [P, HEADS, NT], F32)
        q = sb("b_q", [P, HEADS, NT], F32)
        dmax = sb("b_dmax", [P, HEADS], F32)
        top = sb("b_top", [P, HEADS], F32)
        top_g, top_q = sb("b_top_g", [P, HEADS], F32), sb("b_top_q", [P, HEADS], F32)
        rz = sb("b_rz", [P, TK, 2, 2], F32)
        stats = sb("b_stats", [P, NT, 6], F32)
        mv = sb("b_mv", [P, NT, 2], F32)
        var_eps, half_neg = sb("b_var", [P, NT], F32), sb("b_half", [P, NT], F32)
        rstd, shift = sb("b_rstd", [P, NT], F32), sb("b_shift", [P, NT], F32)
        num = ctx_.enter_context(nc.psum_tensor("b_num", [P, 2, 2, IW], F32))
        den = ctx_.enter_context(nc.psum_tensor("b_den", [P, 2, IW], F32))
        pj = ctx_.enter_context(nc.psum_tensor("b_pj", [P, 2, IW], F32))

        weights_in = sem("b_weights_in")
        adj_in = [sem("b_adj_in0"), sem("b_adj_in1")]
        mask_built = sem("b_mask_built")
        mask_h_used = sem("b_mask_h_used")
        lone_ready = sem("b_lone_ready")
        const_ready = sem("b_const_ready")
        pool_step = sem("b_pool_step")
        wa_step = sem("b_wa_step")
        wx_ready = sem("b_wx_ready")
        x_in = sem("b_x_in")
        out_stored = sem("b_out_stored")
        waited = sem("b_waited")
        stats_made = sem("b_stats_made")
        mv_ready = sem("b_mv_ready")
        rstd_ready = sem("b_rstd_ready")
        shift_ready = sem("b_shift_ready")
        h_ready = sem("b_h_ready")
        prep_ready = sem("b_prep_ready")
        prep_free = sem("b_prep_free")
        s_c_ready = sem("b_s_c_ready")
        dmax_ready = sem("b_dmax_ready")
        top_ready = sem("b_top_ready")
        tops_scaled = sem("b_tops_scaled")
        gq_ready = sem("b_gq_ready")
        u_ready = sem("b_u_ready")
        s_out = sem("b_s_out")
        s_in = [sem(f"b_s_in{i}") for i in range(HEADS)]
        relu_r = sem("b_relu_r")
        r_ready = sem("b_r_ready")
        p_ready = sem("b_p_ready")
        p_used = sem("b_p_used")
        sums_copied = sem("b_sums_copied")
        end_ready = sem("b_end_ready")
        end_free = sem("b_end_free")
        neg_ready = sem("b_neg_ready")
        neg_exp = sem("b_neg_exp")
        elu_step = sem("b_elu_step")
        out_ready = sem("b_out_ready")

        block = ctx_.enter_context(nc.Block())

        def stage(t):
            return p[:, t % 2, :, :].rearrange("p a n -> p (a n)").bitcast(I32)

        def stage_h(t):
            return p[:, 2 + t % 2, 0, :].bitcast(F16)

        @block.sync
        def _(sp):
            sp.dma_start(wx[:, :, 0:F], w.rearrange("(k p) n -> p k n", p=P)).then_inc(weights_in, 16)
            sp.dma_start(a_r[:], a.rearrange("(a n) -> a n", a=1).broadcast_to([P, 2 * D])).then_inc(weights_in, 16)
            for t in range(NT):
                if t >= 2:
                    sp.wait_ge(mask_built, 2 * (t - 1))
                sp.dma_start(stage(t), adjT[t * P:(t + 1) * P, :]).then_inc(adj_in[t % 2], 16)
            sp.sem_inc(out_stored, 16)
            with sp.Fori(0, B) as b:
                sp.wait_ge(out_stored, 16 * b + 16)
                sp.dma_start(xin[:], x1[bass.ds(b, 1), :, :].rearrange("a (t p) f -> p (a t) f", p=P)).then_inc(x_in, 16)
                sp.wait_ge(prep_free, (b + 1) * G_PREP)
                sp.dma_start(s_rows_dram, s_rows[:]).then_inc(s_out, 16)
                sp.wait_ge(s_out, 16 * b + 16)
                for hd in range(HEADS):
                    row = s_rows_dram[hd * NT:(hd + 1) * NT, :].rearrange("(a t) p -> a (t p)", a=1)
                    sp.dma_start(r[:, hd, :], row.broadcast_to([P, N])).then_inc(s_in[hd], 16)
                sp.wait_ge(out_ready, b + 1)
                sp.dma_start(out[bass.ds(b, 1), :, :].rearrange("a (t p) f -> p (a t) f", p=P), xin[:]).then_inc(out_stored, 16)
            sp.wait_ge(out_stored, 16 * (B + 1))

        @block.gpsimd
        def _(pool):
            pool.memset(ident[:], 0.0).then_inc(pool_step, 1)
            pool.memset(half_neg[:], -0.5).then_inc(pool_step, 1)
            pool.memset(ones[:], 1.0).then_inc(const_ready, 1)
            pool.memset(ones_h[:], 1.0).then_inc(const_ready, 1)
            pool.wait_ge(pool_step, 2)
            pool.affine_select(out=ident[:], in_=ident[:], compare_op=ALU.not_equal, fill=1.0, base=0,
                               pattern=[[-1, P]], channel_multiplier=1).then_inc(const_ready, 1)
            with pool.Fori(0, B) as b:
                pool.wait_ge(mv_ready, b + 1)
                pool.sem_inc(waited, 1)
                nc.gpsimd.tensor_scalar(var_eps[:], mv[:, :, 1], EPS, None, ALU.add).then_inc(pool_step, 1)
                pool.wait_ge(pool_step, b + 3)
                nc.gpsimd.tensor_tensor(rstd[:], var_eps[:], half_neg[:], ALU.pow).then_inc(rstd_ready, 1)
                pool.wait_ge(dmax_ready, b + 1)
                pool.sem_inc(waited, 1)
                nc.gpsimd.partition_all_reduce(top[:], dmax[:], P, RMAX).then_inc(top_ready, 1)

        @block.scalar
        def _(act):
            nc.scalar.preload_act_table_set("natural_log_exp_and_others")
            with act.Fori(0, B) as b:
                act.wait_ge(shift_ready, b + 1)
                for t in range(NT):
                    nc.scalar.activation(h[:, t, :], xin[:, t, :], ACT.Relu, bias=shift[:, t:t + 1],
                                         scale=rstd[:, t:t + 1]).then_inc(h_ready, 1)
                for k in range(G_TR):
                    act.wait_ge(prep_ready, b * G_PREP + k + 1)
                    nc.scalar.activation(hT[:, k % KT, (k // KT) * IW:(k // KT + 1) * IW], pj[:, k % 2, :],
                                         ACT.Copy).then_inc(prep_free, 1)
                for t in range(G_PJ):
                    act.wait_ge(prep_ready, b * G_PREP + G_TR + t + 1)
                    nc.scalar.activation(v[:, t, :], pj[:, (G_TR + t) % 2, 0:FX], ACT.Copy).then_inc(prep_free, 1)
                act.wait_ge(prep_ready, b * G_PREP + G_PREP - 1)
                nc.scalar.activation(mean_v[:], pj[0:1, 0, 0:F], ACT.Copy, scale=1.0 / N).then_inc(prep_free, 1)
                act.wait_ge(prep_ready, b * G_PREP + G_PREP)
                nc.scalar.activation(s_rows[:], pj[0:HEADS * NT, 1, 0:P], ACT.Copy).then_inc(prep_free, 1)
                act.wait_ge(tops_scaled, b + 1)
                for hd in range(HEADS):
                    d = v[:, :, F + HEADS + hd]
                    nc.scalar.activation(g[:, hd, :], d, ACT.Exp, bias=top_g[:, hd:hd + 1], scale=ALPHA)
                    last = nc.scalar.activation(q[:, hd, :], d, ACT.Exp, bias=top_q[:, hd:hd + 1], scale=1.0 - ALPHA)
                last.then_inc(gq_ready, 1)
                for hd in range(HEADS):
                    act.wait_ge(s_in[hd], 16 * b + 16)
                    nc.scalar.activation(r[:, hd, :], r[:, hd, :], ACT.Relu, bias=top[:, hd:hd + 1]).then_inc(relu_r, 1)
                    act.wait_ge(relu_r, b * HEADS + hd + 1)
                    nc.scalar.activation(r[:, hd, :], r[:, hd, :], ACT.Exp, scale=ALPHA - 1.0).then_inc(r_ready, 1)
                for n in range(NH):
                    act.wait_ge(p_used, PB + (b * NH + n + 1) * NT)
                    nc.scalar.activation(den_s[:, n % 2, :], den[:, n % 2, :], ACT.Copy).then_inc(sums_copied, 1)
                    nc.scalar.activation(num_s[:, n % 2, :, :], num[:, n % 2, :, :], ACT.Copy).then_inc(sums_copied, 1)
                    act.wait_ge(neg_ready, b * NH + n + 1)
                    nc.scalar.activation(neg[:], neg[:], ACT.Exp).then_inc(neg_exp, 1)

        @block.vector
        def _(dve):
            dve.wait_ge(const_ready, 2)
            for t in range(NT):
                dve.wait_ge(adj_in[t % 2], 16 * (t // 2 + 1))
                nc.vector.tensor_scalar(mask[:, t, :], stage(t), 0.0, None, ALU.is_gt).then_inc(mask_built, 1)
                if t >= 2:
                    dve.wait_ge(mask_h_used, t - 1)
                nc.vector.tensor_scalar(stage_h(t), stage(t), 0.0, None, ALU.is_gt).then_inc(mask_built, 1)
            dve.wait_ge(mask_h_used, NT)
            nc.vector.tensor_scalar(lone[:], num[0:1, :, :, :].rearrange("p a b n -> p (a b n)"), 0.0, None,
                                    ALU.is_equal).then_inc(lone_ready, 1)
            dve.wait_ge(weights_in, 32)
            n = 0
            for kt in range(KT):
                for part in range(2):
                    if n:
                        dve.wait_ge(wa_step, 2 * n)
                    nc.vector.tensor_tensor(wa[:], wx[:, kt, 0:F].rearrange("p (h d) -> p h d", h=HEADS),
                                            spread(a_r[:, part * D:(part + 1) * D], HEADS), ALU.mult).then_inc(wa_step, 1)
                    dve.wait_ge(wa_step, 2 * n + 1)
                    nc.vector.reduce_sum(wx[:, kt, F + part * HEADS:F + (part + 1) * HEADS], wa[:],
                                         axis=AX_X).then_inc(wa_step, 1)
                    n += 1
            dve.wait_ge(wa_step, 2 * n)
            dve.sem_inc(wx_ready, 1)
            dve.sem_inc(end_free, 2 * G_END)

            def weigh(b, n, jt):
                at = (b * NH + n) * NT + jt
                dve.wait_ge(p_used, at + 1)
                cols = slice((n % 2) * HW, (n % 2 + 1) * HW)
                for k in range(2):
                    hd = 2 * (n // 2) + k
                    last = nc.vector.scalar_tensor_tensor(p[:, jt % PB, k, :], r[:, hd, cols], q[:, hd, jt:jt + 1],
                                                          mask[:, jt, cols], ALU.max, ALU.mult)
                last.then_inc(p_ready, 1)

            def finish_sums(b, n):
                m = b * NH + n
                first = n * G_END
                dve.wait_ge(end_ready, m * G_END + 1)
                sums = pj[:, first % 2, :].rearrange("p (k c z) -> p k c z", k=TK, c=4)[:, :, :, 0]
                nc.vector.reciprocal(rz[:].rearrange("p k a c -> p k (a c)"), sums).then_inc(end_free, 1)
                dve.wait_ge(end_free, 2 * G_END + m * G_END + 1)
                for ib in range(2):
                    dve.wait_ge(end_ready, m * G_END + 2 + ib)
                    scale = rz[:, :, :, ib].rearrange("p k (a z) -> p k a z", z=1).broadcast_to([P, TK, 2, D])
                    nc.vector.tensor_tensor(y[:, ib * TK:(ib + 1) * TK, :].rearrange("p k (a d) -> p k a d", a=2),
                                            pj[:, (first + 1 + ib) % 2, :].rearrange("p (k a d) -> p k a d", k=TK, a=2),
                                            scale, ALU.mult).then_inc(end_free, 1)
                dve.wait_ge(end_free, 2 * G_END + (m + 1) * G_END)
                nc.vector.tensor_scalar(neg[:], y[:], 0.0, None, ALU.min).then_inc(neg_ready, 1)

            def finish_elu(b, n):
                m = b * NH + n
                x_part = xin[:, (n % 2) * 2 * TK:(n % 2 + 1) * 2 * TK, (n // 2) * P:(n // 2 + 1) * P]
                dve.wait_ge(neg_exp, m + 1)
                nc.vector.scalar_tensor_tensor(y[:], y[:], 0.0, neg[:], ALU.max, ALU.add).then_inc(elu_step, 1)
                dve.wait_ge(elu_step, 2 * m + 1)
                nc.vector.scalar_tensor_tensor(x_part, y[:], -1.0, x_part, ALU.add, ALU.add).then_inc(elu_step, 1)

            with dve.Fori(0, B) as b:
                dve.wait_ge(x_in, 16 * b + 16)
                for t in range(NT):
                    nc.vector.bn_stats(stats[:, t, :], xin[:, t, :]).then_inc(stats_made, 1)
                dve.wait_ge(stats_made, (b + 1) * NT)
                dve.sem_inc(waited, 1)
                for t in range(NT):
                    last = nc.vector.bn_aggr(mv[:, t, :], stats[:, t, :])
                last.then_inc(mv_ready, 1)
                dve.wait_ge(rstd_ready, b + 1)
                nc.vector.scalar_tensor_tensor(shift[:], mv[:, :, 0], -1.0, rstd[:], ALU.mult,
                                               ALU.mult).then_inc(shift_ready, 1)
                dve.wait_ge(prep_free, b * G_PREP + G_TR + G_PJ)
                nc.vector.tensor_copy(s_c[:].rearrange("p h t -> p t h"), v[:, :, F:F + HEADS]).then_inc(s_c_ready, 1)
                nc.vector.reduce_max(dmax[:], v[:, :, F + HEADS:FX].rearrange("p t h -> p h t"),
                                     axis=AX_X).then_inc(dmax_ready, 1)
                dve.wait_ge(top_ready, b + 1)
                nc.vector.tensor_scalar(top_g[:], top[:], -ALPHA, None, ALU.mult)
                nc.vector.tensor_scalar(top_q[:], top[:], ALPHA - 1.0, None, ALU.mult).then_inc(tops_scaled, 1)
                dve.wait_ge(gq_ready, b + 1)
                for hd in range(HEADS):
                    cols = slice(hd * D, (hd + 1) * D)
                    gain = g[:, hd, :].rearrange("p (t z) -> p t z", z=1)
                    nc.vector.tensor_tensor(h[:, :, cols], v[:, :, cols], gain.broadcast_to([P, NT, D]), ALU.mult)
                    last = nc.vector.tensor_copy(g32[:, :, hd, :], gain.broadcast_to([P, NT, 32]))
                last.then_inc(u_ready, 1)
                for n in range(NH):
                    if n % 2 == 0:
                        dve.wait_ge(r_ready, b * HEADS + n + 2)
                    for jt in range(NT):
                        weigh(b, n, jt)
                        if n and jt == 4:
                            finish_sums(b, n - 1)
                        if n and jt == 8:
                            finish_elu(b, n - 1)
                finish_sums(b, NH - 1)
                finish_elu(b, NH - 1)
                dve.wait_ge(elu_step, 2 * NH * (b + 1))
                dve.sem_inc(out_ready, 1)

        @block.tensor
        def _(pe):
            pe.wait_ge(const_ready, 3)
            for t in range(NT):
                pe.wait_ge(mask_built, 2 * t + 2)
                for k in range(N // IW):
                    last = nc.tensor.matmul(num[0:1, k // 2, k % 2, :], ones_h[:], stage_h(t)[:, k * IW:(k + 1) * IW],
                                            start=(t == 0), stop=(t == NT - 1))
                last.then_inc(mask_h_used, 1)
            pe.wait_ge(lone_ready, 1)
            pe.wait_ge(wx_ready, 1)
            pe.sem_inc(p_used, PB)

            def group(b, k):
                if k >= 2:
                    pe.wait_ge(prep_free, b * G_PREP + k - 1)

            def finish(b, n):
                m = b * NH + n
                for k in range(G_END):
                    if k < 2:
                        if n == 0:
                            pe.wait_ge(prep_free, (b + 1) * G_PREP)
                        else:
                            pe.wait_ge(end_free, 2 * G_END + (m - 1) * G_END + k + 2)
                    else:
                        pe.wait_ge(end_free, 2 * G_END + m * G_END + k - 1)
                    if k < 2:
                        pe.wait_ge(sums_copied, 2 * m + 1 + k)
                    src = den_s[:, n % 2, :] if k == 0 else num_s[:, n % 2, k - 1, :]
                    for i in range(TK):
                        last = nc.tensor.transpose(pj[:, (n * G_END + k) % 2, i * P:(i + 1) * P],
                                                   src[:, i * P:(i + 1) * P], ident[:])
                    last.then_inc(end_ready, 1)

            with pe.Fori(0, B) as b:
                pe.wait_ge(end_free, 2 * G_END + b * NH * G_END)
                for k in range(G_TR):
                    group(b, k)
                    pe.wait_ge(h_ready, b * NT + 4 * (k // KT) + 4)
                    for i in range(4):
                        t = 4 * (k // KT) + i
                        last = nc.tensor.transpose(pj[:, k % 2, i * P:(i + 1) * P],
                                                   h[:, t, (k % KT) * P:(k % KT + 1) * P], ident[:])
                    last.then_inc(prep_ready, 1)
                pe.wait_ge(prep_free, b * G_PREP + G_TR)
                for t in range(G_PJ):
                    group(b, G_TR + t)
                    for kt in range(KT):
                        last = nc.tensor.matmul(pj[:, (G_TR + t) % 2, 0:FX], hT[:, kt, t * P:(t + 1) * P],
                                                wx[:, kt, :], start=(kt == 0), stop=(kt == KT - 1))
                    last.then_inc(prep_ready, 1)
                pe.wait_ge(prep_free, b * G_PREP + G_TR + G_PJ)
                for t in range(NT):
                    last = nc.tensor.matmul(pj[0:1, 0, 0:F], ones[:, 0:1], v[:, t, 0:F],
                                            start=(t == 0), stop=(t == NT - 1))
                last.then_inc(prep_ready, 1)
                pe.wait_ge(s_c_ready, b + 1)
                pe.sem_inc(waited, 1)
                nc.tensor.transpose(pj[0:HEADS * NT, 1, 0:P], s_c[:].rearrange("p h t -> p (h t)"),
                                    ident[:]).then_inc(prep_ready, 1)
                pe.wait_ge(prep_free, (b + 1) * G_PREP)
                pe.wait_ge(u_ready, b + 1)
                for n in range(NH):
                    s, pr = n % 2, n // 2
                    rows = (n % 2) * HW
                    if n >= 2:
                        pe.wait_ge(sums_copied, 2 * (b * NH + n - 1))
                    for ib in range(2):
                        alone = lone[0:1, rows + ib * IW:rows + (ib + 1) * IW]
                        for k in range(2):
                            nc.tensor.matmul(num[k * D:(k + 1) * D, s, ib, :],
                                             mean_v[0:1, pr * P + k * D:pr * P + (k + 1) * D], alone,
                                             start=True, stop=False)
                    for ib in range(2):
                        alone = lone[0:1, rows + ib * IW:rows + (ib + 1) * IW]
                        for k in range(2):
                            c = 2 * k + ib
                            nc.tensor.matmul(den[c * 32:(c + 1) * 32, s, :], ones[0:1, :], alone,
                                             start=True, stop=False)
                    for jt in range(NT):
                        end = jt == NT - 1
                        pe.wait_ge(p_ready, (b * NH + n) * NT + jt + 1)
                        for ib in range(2):
                            for k in range(2):
                                nc.tensor.matmul(num[k * D:(k + 1) * D, s, ib, :],
                                                 h[:, jt, pr * P + k * D:pr * P + (k + 1) * D],
                                                 p[:, jt % PB, k, ib * IW:(ib + 1) * IW], start=False, stop=end)
                        for ib in range(2):
                            for k in range(2):
                                c = 2 * k + ib
                                last = nc.tensor.matmul(den[c * 32:(c + 1) * 32, s, :], g32[:, jt, 2 * pr + k, :],
                                                        p[:, jt % PB, k, ib * IW:(ib + 1) * IW],
                                                        start=False, stop=end)
                        last.then_inc(p_used, 1)
                        if n and jt == 2:
                            finish(b, n - 1)
                finish(b, NH - 1)


def kernel(**inputs):
    import numpy as _np
    import concourse.bacc as _bacc
    from concourse import mybir as _mybir
    from concourse.bass_utils import run_bass_kernel_spmd as _run

    nc = _bacc.Bacc("TRN2", target_bir_lowering=False, num_devices=1)
    arrays = {}

    def put(name, a):
        a = _np.ascontiguousarray(a)
        arrays[name] = a
        return nc.dram_tensor(name, a.shape, _mybir.dt.from_np(a.dtype), kind="ExternalInput").ap()

    x = _np.asarray(inputs["x"])
    B, N, F = x.shape
    f32 = _mybir.dt.float32
    x_d = put("x", x)
    adjT = put("adjT", _np.asarray(inputs["adj"]).T)
    wT = {k: put(f"w{k}T", _np.asarray(inputs[f"L0_gnn_W{k}"]).T) for k in "qkvo"}
    bc = {k: put(f"b{k}", _np.asarray(inputs[f"L0_gnn_b{k}"]).reshape(F // P, P).T) for k in "qk"}
    br = {k: put(f"b{k}", inputs[f"L0_gnn_b{k}"]) for k in "vo"}
    gamma, beta = put("gamma", inputs["L0_gnn_gamma"]), put("beta", inputs["L0_gnn_beta"])
    w1, a1 = put("w1", inputs["L1_gnn_W"]), put("a1", inputs["L1_gnn_a"])
    x1 = nc.dram_tensor("x1", (B, N, F), f32, kind="Internal").ap()
    s_rows = nc.dram_tensor("s_rows", (4 * N // P, P), f32, kind="Internal").ap()
    out = nc.dram_tensor("out", (B, N, F), f32, kind="ExternalOutput").ap()
    layer0(nc, x_d, adjT, wT["q"], bc["q"], wT["k"], bc["k"], wT["v"], br["v"], wT["o"], br["o"], gamma, beta, x1)
    layer1(nc, x1, adjT, w1, a1, s_rows, out)
    r = _run(nc, [arrays], core_ids=[0])
    return r.results[0]["out"]
```

```python
import math

import concourse.bass as bass
from concourse import mybir
from contextlib import ExitStack

ALU = mybir.AluOpType
ACT = mybir.ActivationFunctionType
AX_X = mybir.AxisListType.X
F32 = mybir.dt.float32
F16 = mybir.dt.float16
I32 = mybir.dt.int32
U8 = mybir.dt.uint8
RMAX = bass.bass_isa.ReduceOp.max

P = 128
IW = 512
CHUNK = 256
CLIP = 10.0
EPS = 1e-5
ALPHA = 0.2
LAG = 2
EBUF = 4


def spread(ap, n):
    p, m = ap.shape
    return ap.rearrange("p (a m) -> p a m", a=1).broadcast_to([p, n, m])


def layer0(nc, x, adjT, wqT, bq, wkT, bk, wvT, bv, woT, bo, gamma, beta, x1):
    B, N, F = x.shape
    NT = N // P
    KT = F // P
    D = F // 4
    PAIRS = F // (2 * D)
    IB = N // IW
    NCH = N // CHUNK
    JC = CHUNK // P
    assert PAIRS == KT == 2 and 2 * D == P and JC == 2 and NT % EBUF == 0
    LO, HI = math.exp(-CLIP), math.exp(CLIP)

    G_TR, G_V, G_QK, G_WO = KT * NT // 4, NT // 2, 2 * IB, NT // 2
    G_FIRST = G_TR + G_QK + G_V
    G_B = G_QK + G_TR + G_WO + G_QK + G_V
    T_IB, T_PR, T_B = NT, IB * NT, PAIRS * IB * NT
    C_IB, C_PR, C_B = NCH, IB * NCH, PAIRS * IB * NCH
    S_K, S_Q = 8 * 16, 4 * 16

    with ExitStack() as ctx_:
        def sb(name, shape, dt):
            return ctx_.enter_context(nc.sbuf_tensor(name, shape, dt))

        def sem(name):
            return ctx_.enter_context(nc.semaphore(name))

        mask = sb("a_mask", [P, NT, N], U8)
        h = sb("a_h", [P, NT, F], F32)
        xr = sb("a_xr", [P, NT, F], F32)
        o = sb("a_o", [P, NT, F], F32)
        hT = sb("a_hT", [P, KT, N], F32)
        v = sb("a_v", [P, NT, F], F32)
        ctxT = sb("a_ctxT", [P, PAIRS, N], F32)
        q_st = sb("a_q_st", [P, 2, N], F16)
        kh_st = sb("a_kh_st", [P, 2, N], F16)
        kl_st = sb("a_kl_st", [P, 2, N], F16)
        q_hi, q_lo = sb("a_q_hi", [P, N], F16), sb("a_q_lo", [P, N], F16)
        k_hi, k_lo = sb("a_k_hi", [P, N], F16), sb("a_k_lo", [P, N], F16)
        e = sb("a_e", [P, EBUF, 2, IW], F32)
        wq, wk = sb("a_wq", [P, KT, F], F32), sb("a_wk", [P, KT, F], F32)
        wv, wo = sb("a_wv", [P, KT, F], F32), sb("a_wo", [P, KT, F], F32)
        bq_c, bk_c = sb("a_bq", [P, PAIRS], F32), sb("a_bk", [P, PAIRS], F32)
        bv_r, bo_r = sb("a_bv", [P, F], F32), sb("a_bo", [P, F], F32)
        gamma_r, beta_r = sb("a_gamma", [P, F], F32), sb("a_beta", [P, F], F32)
        rz = sb("a_rz", [P, 2, IW], F32)
        ident = sb("a_ident", [P, P], F32)
        ones = sb("a_ones", [P, D], F32)
        half_neg = sb("a_half", [P, NT], F32)
        stats = sb("a_stats", [P, NT, 6], F32)
        var_eps = sb("a_var", [P, NT], F32)
        mv_x, mv_o = sb("a_mv_x", [P, NT, 2], F32), sb("a_mv_o", [P, NT, 2], F32)
        rstd_x, shift_x = sb("a_rstd_x", [P, NT], F32), sb("a_shift_x", [P, NT], F32)
        rstd_r, shift_r = sb("a_rstd_r", [P, NT], F32), sb("a_shift_r", [P, NT], F32)
        rstd_o = sb("a_rstd_o", [P, NT], F32)
        sc = ctx_.enter_context(nc.psum_tensor("a_sc", [P, 4, IW], F32))
        num = ctx_.enter_context(nc.psum_tensor("a_num", [P, 2, IW], F32))
        den = ctx_.enter_context(nc.psum_tensor("a_den", [P, 2, IW], F32))

        weights_in = sem("a_weights_in")
        adj_in = [sem("a_adj_in0"), sem("a_adj_in1")]
        mask_built = sem("a_mask_built")
        const_ready = sem("a_const_ready")
        x_in = sem("a_x_in")
        xr_in = sem("a_xr_in")
        x1_stored = sem("a_x1_stored")
        stats_made = sem("a_stats_made")
        waited = sem("a_waited")
        mv_ready = sem("a_mv_ready")
        pool_step = sem("a_pool_step")
        rstd_ready = sem("a_rstd_ready")
        shift_ready = sem("a_shift_ready")
        kept = sem("a_kept")
        h_ready = sem("a_h_ready")
        o_ready = sem("a_o_ready")
        bias_added = sem("a_bias_added")
        group_ready = sem("a_group_ready")
        group_free = sem("a_group_free")
        hi_ready = sem("a_hi_ready")
        k_stacked, q_stacked = sem("a_k_stacked"), sem("a_q_stacked")
        scores_ready = sem("a_scores_ready")
        exp_ready = sem("a_exp_ready")
        masked = sem("a_masked")
        p_ready = sem("a_p_ready")
        p_used = sem("a_p_used")
        ln_ready = sem("a_ln_ready")
        rz_ready = sem("a_rz_ready")
        chunk_free = sem("a_chunk_free")
        ctx_added = sem("a_ctx_added")
        ctx_done = sem("a_ctx_done")
        post_step = sem("a_post_step")
        out_ready = sem("a_out_ready")

        block = ctx_.enter_context(nc.Block())

        def stage(t):
            return e[:, 2 * (t % 2):2 * (t % 2) + 2, :, :].rearrange("p a b n -> p (a b n)").bitcast(I32)

        def rows_of(dram, b):
            return dram[bass.ds(b, 1), :, :].rearrange("a (t p) f -> p (a t) f", p=P)

        def g_qk1(b):
            return b * G_B + G_FIRST

        def g_tr_next(b):
            return b * G_B + G_FIRST + G_QK

        def g_wo(b, nxt):
            return b * G_B + G_FIRST + G_QK + (G_TR if nxt else 0)

        def g_qk_next(b):
            return b * G_B + G_FIRST + G_QK + G_TR + G_WO

        def g_v_next(b):
            return b * G_B + G_FIRST + G_QK + G_TR + G_WO + G_QK

        @block.sync
        def _(sp):
            sp.dma_start(h[:], rows_of(x, 0)).then_inc(x_in, 16)
            for w, src in ((wq, wqT), (wk, wkT), (wv, wvT), (wo, woT)):
                sp.dma_start(w[:], src.rearrange("(k p) n -> p k n", p=P)).then_inc(weights_in, 16)
            for c, src in ((bq_c, bq), (bk_c, bk)):
                sp.dma_start(c[:], src).then_inc(weights_in, 16)
            for r, src in ((bv_r, bv), (bo_r, bo), (gamma_r, gamma), (beta_r, beta)):
                sp.dma_start(r[:], src.rearrange("(a n) -> a n", a=1).broadcast_to([P, F])).then_inc(weights_in, 16)
            for t in range(NT):
                if t >= 2:
                    sp.wait_ge(mask_built, t - 1)
                sp.dma_start(stage(t), adjT[t * P:(t + 1) * P, :]).then_inc(adj_in[t % 2], 16)

            def stack(g):
                sp.wait_ge(group_free, g + 4 + IB)
                for hd in range(2):
                    mine = slice(hd * D, (hd + 1) * D)
                    for dst, src in ((kh_st, k_hi), (kl_st, k_lo)):
                        sp.dma_start(dst[0:D, hd, :], src[mine, :]).then_inc(k_stacked, 16)
                        sp.dma_start(dst[D:P, hd, :], src[mine, :]).then_inc(k_stacked, 16)
                sp.wait_ge(group_free, g + 4 + 2 * IB)
                for hd in range(2):
                    mine = slice(hd * D, (hd + 1) * D)
                    sp.dma_start(q_st[0:D, hd, :], q_hi[mine, :]).then_inc(q_stacked, 16)
                    sp.dma_start(q_st[D:P, hd, :], q_lo[mine, :]).then_inc(q_stacked, 16)

            def batch(b, nxt):
                sp.dma_start(xr[:], rows_of(x, b)).then_inc(xr_in, 16)
                if nxt:
                    sp.dma_start(h[:], rows_of(x, b + 1)).then_inc(x_in, 16)
                stack(g_qk1(b))
                if nxt:
                    stack(g_qk_next(b))
                sp.wait_ge(out_ready, b + 1)
                sp.dma_start(rows_of(x1, b), o[:]).then_inc(x1_stored, 16)

            sp.sem_inc(x1_stored, 16)
            stack(G_TR)
            with sp.Fori(0, B - 1) as b:
                batch(b, True)
            batch(B - 1, False)
            sp.wait_ge(x1_stored, 16 * (B + 1))

        @block.gpsimd
        def _(pool):
            pool.memset(ident[:], 0.0).then_inc(pool_step, 1)
            pool.memset(ones[:], 1.0).then_inc(const_ready, 1)
            pool.memset(half_neg[:], -0.5).then_inc(pool_step, 1)
            pool.wait_ge(pool_step, 2)
            pool.affine_select(out=ident[:], in_=ident[:], compare_op=ALU.not_equal, fill=1.0, base=0,
                               pattern=[[-1, P]], channel_multiplier=1).then_inc(const_ready, 1)
            pool.wait_ge(weights_in, 160)

            def make_rstd(k, mv, rstd):
                pool.wait_ge(mv_ready, k + 1)
                pool.sem_inc(waited, 1)
                nc.gpsimd.tensor_scalar(var_eps[:], mv[:, :, 1], EPS, None, ALU.add).then_inc(pool_step, 1)
                pool.wait_ge(pool_step, k + 3)
                nc.gpsimd.tensor_tensor(rstd[:], var_eps[:], half_neg[:], ALU.pow).then_inc(rstd_ready, 1)

            def batch(b, nxt):
                if nxt:
                    make_rstd(2 * b + 1, mv_x, rstd_x)
                pool.wait_ge(o_ready, (b + 1) * NT)
                nc.gpsimd.tensor_tensor(o[:], o[:], spread(bo_r[:], NT), ALU.add).then_inc(bias_added, 1)
                nc.gpsimd.tensor_tensor(xr[:], xr[:], spread(beta_r[:], NT), ALU.add).then_inc(bias_added, 1)
                make_rstd(2 * b + (2 if nxt else 1), mv_o, rstd_o)

            make_rstd(0, mv_x, rstd_x)
            with pool.Fori(0, B - 1) as b:
                batch(b, True)
            batch(B - 1, False)

        @block.scalar
        def _(act):
            nc.scalar.preload_act_table_set("natural_log_exp_and_others")

            def make_h(t):
                nc.scalar.activation(h[:, t, :], h[:, t, :], ACT.Relu, bias=shift_x[:, t:t + 1],
                                     scale=rstd_x[:, t:t + 1]).then_inc(h_ready, 1)

            def make_o(t):
                nc.scalar.activation(o[:, t, :], xr[:, t, :], ACT.Relu, bias=shift_r[:, t:t + 1],
                                     scale=rstd_r[:, t:t + 1]).then_inc(o_ready, 1)

            def high_halves(first, pr):
                for g in range(G_QK):
                    to, bias = ((k_hi, bk_c), (q_hi, bq_c))[g // IB]
                    act.wait_ge(group_ready, first + g + 1)
                    nc.scalar.activation(to[:, (g % IB) * IW:(g % IB + 1) * IW], sc[:, g % 4, :], ACT.Identity,
                                         bias=bias[:, pr:pr + 1]).then_inc(hi_ready, 1)

            def invert(done, c):
                act.wait_ge(p_used, EBUF + JC * (done + 1))
                act.wait_ge(ctx_added, done + 1)
                nc.scalar.activation(rz[:, c, :], den[:, c, :], ACT.Ln).then_inc(ln_ready, 1)
                act.wait_ge(ln_ready, done + 1)
                nc.scalar.activation(rz[:, c, :], rz[:, c, :], ACT.Exp, scale=-1.0).then_inc(rz_ready, 1)

            def attend(b, pr, nxt):
                t0, c0 = b * T_B + pr * T_PR, b * C_B + pr * C_PR

                def block_of(ib, first):
                    for jt in range(NT):
                        at = t0 + ib * T_IB + jt
                        act.wait_ge(scores_ready, at + 1)
                        act.wait_ge(p_used, at + 1)
                        nc.scalar.activation(e[:, jt % EBUF, :, :], sc[:, 2 * (jt % 2):2 * (jt % 2) + 2, :],
                                             ACT.Exp, scale=float(D) ** -0.5).then_inc(exp_ready, 1)
                        if first and pr == 1:
                            if nxt:
                                make_h(jt)
                            make_o(jt)
                        if jt % JC == 0 and not (first and jt < LAG * JC):
                            invert(c0 + ib * C_IB + jt // JC - LAG, (jt // JC) % 2)

                if pr == 1:
                    act.wait_ge(xr_in, 16 * b + 16)
                    act.wait_ge(kept, b + 1)
                    if nxt:
                        act.wait_ge(shift_ready, b + 2)
                block_of(0, True)
                with act.Fori(1, IB) as ib:
                    block_of(ib, False)
                for c in range(LAG):
                    invert(c0 + C_PR - LAG + c, c % 2)

            def batch(b, nxt):
                attend(b, 0, nxt)
                high_halves(g_qk1(b), 1)
                act.wait_ge(x1_stored, 16 * b + 16)
                attend(b, 1, nxt)
                if nxt:
                    high_halves(g_qk_next(b), 0)

            act.wait_ge(shift_ready, 1)
            for t in range(NT):
                make_h(t)
            act.wait_ge(weights_in, 160)
            high_halves(G_TR, 0)
            act.wait_ge(mask_built, NT)
            with act.Fori(0, B - 1) as b:
                batch(b, True)
            batch(B - 1, False)

        @block.vector
        def _(dve):
            dve.sem_inc(group_free, 4)
            dve.sem_inc(chunk_free, 2)
            dve.sem_inc(ctx_added, 2)

            def stats_of(src, t):
                nc.vector.bn_stats(stats[:, t, :], src[:, t, :]).then_inc(stats_made, 1)

            def aggregate(k, mv):
                dve.wait_ge(stats_made, (k + 1) * NT)
                dve.sem_inc(waited, 1)
                for t in range(NT):
                    last = nc.vector.bn_aggr(mv[:, t, :], stats[:, t, :])
                last.then_inc(mv_ready, 1)

            def make_shift(k):
                dve.wait_ge(rstd_ready, k + 1)
                nc.vector.scalar_tensor_tensor(shift_x[:], mv_x[:, :, 0], -1.0, rstd_x[:], ALU.mult,
                                               ALU.mult).then_inc(shift_ready, 1)

            def keep():
                nc.vector.tensor_copy(rstd_r[:], rstd_x[:])
                nc.vector.tensor_copy(shift_r[:], shift_x[:]).then_inc(kept, 1)

            def move_hT(first):
                for g in range(G_TR):
                    dve.wait_ge(group_ready, first + g + 1)
                    nc.vector.tensor_copy(hT[:, g % KT, (g // KT) * IW:(g // KT + 1) * IW],
                                          sc[:, g % 4, :]).then_inc(group_free, 1)

            def low_half(first, g, pr, halves):
                hi, lo, bias = ((k_hi, k_lo, bk_c), (q_hi, q_lo, bq_c))[g // IB]
                cols = slice((g % IB) * IW, (g % IB + 1) * IW)
                dve.wait_ge(hi_ready, halves + g + 1)
                nc.vector.scalar_tensor_tensor(lo[:, cols], sc[:, g % 4, :], bias[:, pr:pr + 1],
                                               hi[:, cols], ALU.add, ALU.subtract).then_inc(group_free, 1)

            def move_v(first, g):
                dve.wait_ge(group_ready, first + g + 1)
                nc.vector.tensor_tensor(v[:, 2 * g:2 * g + 2, :], sc[:, g % 4, :].rearrange("p (a f) -> p a f", a=2),
                                        spread(bv_r[:], 2), ALU.add).then_inc(group_free, 1)

            def weigh(at, ib, jt):
                slot = e[:, jt % EBUF, :, :]
                dve.wait_ge(exp_ready, at + 1)
                nc.vector.scalar_tensor_tensor(slot, slot, HI, spread(mask[:, jt, bass.ds(ib * IW, IW)], 2),
                                               ALU.min, ALU.mult).then_inc(masked, 1)
                dve.wait_ge(masked, at + 1)
                nc.vector.tensor_scalar(slot, slot, LO, None, ALU.max).then_inc(p_ready, 1)

            def normalise(done, c, cols, fresh):
                dve.wait_ge(rz_ready, done + 1)
                nc.vector.tensor_tensor(rz[:, c, :], num[:, c, :], rz[:, c, :], ALU.mult).then_inc(chunk_free, 1)
                dve.wait_ge(chunk_free, done + 3)
                if fresh:
                    nc.vector.tensor_copy(cols, rz[:, c, :]).then_inc(ctx_added, 1)
                else:
                    nc.vector.tensor_tensor(cols, cols, rz[:, c, :], ALU.add).then_inc(ctx_added, 1)

            def attend(b, pr, nxt):
                t0, c0 = b * T_B + pr * T_PR, b * C_B + pr * C_PR

                def block_of(ib, first):
                    for jt in range(NT):
                        weigh(t0 + ib * T_IB + jt, ib, jt)
                        if first and pr == 0 and nxt:
                            if jt == 0:
                                dve.wait_ge(x_in, 16 * b + 32)
                            stats_of(h, jt)
                        if jt % JC == 0 and not (first and jt < LAG * JC):
                            c = jt // JC - LAG
                            cols = ctxT[:, pr, bass.ds((ib if c >= 0 else ib - 1) * IW, IW)]
                            normalise(c0 + ib * C_IB + c, c % 2, cols, c == 0)

                block_of(0, True)
                if pr == 0 and nxt:
                    aggregate(2 * b + 1, mv_x)
                with dve.Fori(1, IB) as ib:
                    block_of(ib, False)
                for c in range(NCH - LAG, NCH):
                    normalise(c0 + C_PR - NCH + c, c % 2, ctxT[:, pr, N - IW:N], False)
                if pr == 0 and nxt:
                    make_shift(2 * b + 1)

            def centre(t):
                nc.vector.scalar_tensor_tensor(o[:, t, :], o[:, t, :], mv_o[:, t, 0:1], gamma_r[:], ALU.subtract,
                                               ALU.mult).then_inc(post_step, 1)

            def finish(t):
                return nc.vector.scalar_tensor_tensor(o[:, t, :], o[:, t, :], rstd_o[:, t:t + 1], xr[:, t, :],
                                                      ALU.mult, ALU.add)

            def batch(b, nxt):
                attend(b, 0, nxt)
                for g in range(G_QK):
                    low_half(g_qk1(b), g, 1, (2 * b + 1) * G_QK)
                attend(b, 1, nxt)
                nc.vector.drain().then_inc(ctx_done, 1)
                if nxt:
                    dve.wait_ge(h_ready, (b + 2) * NT)
                    move_hT(g_tr_next(b))
                dve.wait_ge(bias_added, 2 * b + 2)
                for g in range(G_WO):
                    dve.wait_ge(group_ready, g_wo(b, nxt) + g + 1)
                    rows = o[:, 2 * g:2 * g + 2, :]
                    nc.vector.tensor_tensor(rows, sc[:, g % 4, :].rearrange("p (a f) -> p a f", a=2), rows,
                                            ALU.add).then_inc(group_free, 1)
                    if g:
                        dve.wait_ge(group_free, g_wo(b, nxt) + g + 4)
                        stats_of(o, 2 * g - 2)
                        stats_of(o, 2 * g - 1)
                dve.wait_ge(group_free, g_wo(b, nxt) + G_WO + 4)
                stats_of(o, NT - 2)
                stats_of(o, NT - 1)
                k = 2 * b + (2 if nxt else 1)
                aggregate(k, mv_o)
                dve.wait_ge(mv_ready, k + 1)
                if nxt:
                    keep()
                    for g in range(G_QK):
                        low_half(g_qk_next(b), g, 0, (2 * b + 2) * G_QK)
                        centre(2 * g)
                        centre(2 * g + 1)
                    dve.wait_ge(rstd_ready, k + 1)
                    for g in range(G_V):
                        move_v(g_v_next(b), g)
                        dve.wait_ge(post_step, b * NT + 2 * g + 2)
                        finish(2 * g)
                        last = finish(2 * g + 1)
                else:
                    for t in range(NT):
                        centre(t)
                    dve.wait_ge(rstd_ready, k + 1)
                    for t in range(NT):
                        dve.wait_ge(post_step, b * NT + t + 1)
                        last = finish(t)
                last.then_inc(out_ready, 1)

            dve.wait_ge(x_in, 16)
            for t in range(NT):
                stats_of(h, t)
            aggregate(0, mv_x)
            make_shift(0)
            dve.wait_ge(shift_ready, 1)
            keep()
            for t in range(NT):
                dve.wait_ge(adj_in[t % 2], 16 * (t // 2 + 1))
                nc.vector.tensor_scalar(mask[:, t, :], stage(t), 0.0, None, ALU.not_equal).then_inc(mask_built, 1)
            dve.wait_ge(weights_in, 160)
            move_hT(0)
            for g in range(G_QK):
                low_half(G_TR, g, 0, 0)
            for g in range(G_V):
                move_v(G_TR + G_QK, g)
            with dve.Fori(0, B - 1) as b:
                batch(b, True)
            batch(B - 1, False)

        @block.tensor
        def _(pe):
            pe.wait_ge(const_ready, 2)
            pe.sem_inc(p_used, EBUF)

            def group(g):
                pe.wait_ge(group_free, g + 1)

            def transpose_h(first, tiles):
                for g in range(G_TR):
                    group(first + g)
                    pe.wait_ge(h_ready, tiles + 4 * (g // KT) + 4)
                    for k in range(4):
                        t = 4 * (g // KT) + k
                        last = nc.tensor.transpose(sc[:, g % 4, k * P:(k + 1) * P],
                                                   h[:, t, (g % KT) * P:(g % KT + 1) * P], ident[:])
                    last.then_inc(group_ready, 1)

            def project_qk(first, pr):
                for g in range(G_QK):
                    group(first + g)
                    w = (wk, wq)[g // IB]
                    for kt in range(KT):
                        last = nc.tensor.matmul(sc[:, g % 4, :], w[:, kt, pr * P:(pr + 1) * P],
                                                hT[:, kt, (g % IB) * IW:(g % IB + 1) * IW],
                                                start=(kt == 0), stop=(kt == KT - 1))
                    last.then_inc(group_ready, 1)

            def project_v(first):
                for g in range(G_V):
                    group(first + g)
                    for k in range(2):
                        t = 2 * g + k
                        for kt in range(KT):
                            last = nc.tensor.matmul(sc[:, g % 4, k * F:(k + 1) * F], hT[:, kt, t * P:(t + 1) * P],
                                                    wv[:, kt, :], start=(kt == 0), stop=(kt == KT - 1))
                    last.then_inc(group_ready, 1)

            def project_context(first):
                for g in range(G_WO):
                    group(first + g)
                    for k in range(2):
                        t = 2 * g + k
                        for pr in range(PAIRS):
                            last = nc.tensor.matmul(sc[:, g % 4, k * F:(k + 1) * F], ctxT[:, pr, t * P:(t + 1) * P],
                                                    wo[:, pr, :], start=(pr == 0), stop=(pr == PAIRS - 1))
                    last.then_inc(group_ready, 1)

            def score(ib, jt):
                rows = slice(jt * P, (jt + 1) * P)
                for hd in range(2):
                    out = sc[:, 2 * (jt % 2) + hd, :]
                    q = q_st[:, hd, bass.ds(ib * IW, IW)]
                    nc.tensor.matmul(out, kh_st[:, hd, rows], q, start=True, stop=False)
                    last = nc.tensor.matmul(out, kl_st[:, hd, rows], q, start=False, stop=True)
                last.then_inc(scores_ready, 1)

            def apply(at, done, jt, pr):
                c = (jt // JC) % 2
                if jt % JC == 0:
                    pe.wait_ge(chunk_free, done + 1)
                pe.wait_ge(p_ready, at + 1)
                first, final = jt % JC == 0, jt % JC == JC - 1
                for hd in range(2):
                    nc.tensor.matmul(num[hd * D:(hd + 1) * D, c, :],
                                     v[:, jt, pr * P + hd * D:pr * P + (hd + 1) * D],
                                     e[:, jt % EBUF, hd, :], start=first, stop=final)
                for hd in range(2):
                    last = nc.tensor.matmul(den[hd * D:(hd + 1) * D, c, :], ones[:],
                                            e[:, jt % EBUF, hd, :], start=first, stop=final)
                last.then_inc(p_used, 1)

            def attend(b, pr):
                t0, c0 = b * T_B + pr * T_PR, b * C_B + pr * C_PR
                pe.wait_ge(k_stacked, (b * PAIRS + pr + 1) * S_K)
                pe.wait_ge(q_stacked, (b * PAIRS + pr + 1) * S_Q)
                score(0, 0)
                score(0, 1)

                def block_of(ib, last):
                    for jt in range(NT):
                        at = t0 + ib * T_IB + jt
                        if jt + 2 < NT or not last:
                            pe.wait_ge(exp_ready, at + 1)
                            score(ib + (jt + 2) // NT, (jt + 2) % NT)
                        apply(at, c0 + ib * C_IB + jt // JC, jt, pr)

                with pe.Fori(0, IB - 1) as ib:
                    block_of(ib, False)
                block_of(IB - 1, True)

            def batch(b, nxt):
                pe.wait_ge(group_free, g_qk1(b) + 4)
                attend(b, 0)
                project_qk(g_qk1(b), 1)
                pe.wait_ge(group_free, g_qk1(b) + G_QK + 4)
                attend(b, 1)
                if nxt:
                    transpose_h(g_tr_next(b), (b + 1) * NT)
                pe.wait_ge(ctx_done, b + 1)
                project_context(g_wo(b, nxt))
                if nxt:
                    pe.wait_ge(group_free, g_tr_next(b) + G_TR + 4)
                    project_qk(g_qk_next(b), 0)
                    project_v(g_v_next(b))

            transpose_h(0, 0)
            pe.wait_ge(weights_in, 160)
            pe.wait_ge(group_free, G_TR + 4)
            project_qk(G_TR, 0)
            project_v(G_TR + G_QK)
            with pe.Fori(0, B - 1) as b:
                batch(b, True)
            batch(B - 1, False)


def layer1(nc, x1, adjT, w, a, s_dram, out):
    B, N, F = x1.shape
    NT, KT, D = N // P, F // P, F // 4
    HEADS = F // D
    HW = 2 * IW
    FX = F + 2 * HEADS
    NH = KT * N // HW
    TB = NH * NT
    PB = 4
    TK = IW // P
    G_TR, G_PJ = KT * NT // 4, NT
    G_PREP = G_TR + G_PJ + 2
    G_END = 3
    ROWS, MEAN = G_PREP - 2, G_PREP - 1
    assert NH == 4 and KT == 2 and NT == 16

    behind = {t: [] for t in range(TB)}
    for n in range(NH):
        for k in range(G_END):
            behind[n * NT + 2 + k].append(("end", n - 1, k))
    for i, t in enumerate((31, 32, 33, 37)):
        behind[t] += [("prep", 2 * i), ("prep", 2 * i + 1)]
    for i in range(G_PJ // 2):
        behind[38 + i] += [("prep", G_TR + 2 * i), ("prep", G_TR + 2 * i + 1)]
    behind[49].append(("prep", ROWS))
    behind[53].append(("prep", MEAN))
    order = [g for t in range(TB) for g in behind[t]]

    with ExitStack() as ctx_:
        def sb(name, shape, dt):
            return ctx_.enter_context(nc.sbuf_tensor(name, shape, dt))

        def sem(name):
            return ctx_.enter_context(nc.semaphore(name))

        mask = sb("b_mask", [P, NT, N], U8)
        hv = sb("b_hv", [P, NT, F], F32)
        u = sb("b_u", [P, NT, F], F32)
        hT = sb("b_hT", [P, KT, N], F32)
        sd = sb("b_sd", [P, NT, 2 * HEADS], F32)
        g32 = sb("b_g32", [P, NT, HEADS, 32], F32)
        r = sb("b_r", [P, HEADS, N], F32)
        p = sb("b_p", [P, PB, 2, HW], F32)
        xr = sb("b_xr", [P, 2, 2 * TK, P], F32)
        num_s = sb("b_num_s", [P, 2, 2, IW], F32)
        den_s = sb("b_den_s", [P, 2, IW], F32)
        y = sb("b_y", [P, 2 * TK, P], F32)
        neg = sb("b_neg", [P, 2 * TK, P], F32)
        wx = sb("b_wx", [P, KT, FX], F32)
        a_r = sb("b_a", [P, 2 * D], F32)
        wa = sb("b_wa", [P, HEADS, D], F32)
        ident = sb("b_ident", [P, P], F32)
        ones = sb("b_ones", [P, 32], F32)
        ones_h = sb("b_ones_h", [P, 1], F16)
        lone = sb("b_lone", [1, N], F32)
        mean_v = sb("b_mean_v", [1, F], F32)
        s_c = sb("b_s_c", [P, HEADS, NT], F32)
        s_rows = sb("b_s_rows", [HEADS * NT, P], F32)
        g = sb("b_g", [P, HEADS, NT], F32)
        q, q_next = sb("b_q", [P, HEADS, NT], F32), sb("b_q_next", [P, HEADS, NT], F32)
        dmax = sb("b_dmax", [P, HEADS], F32)
        top = sb("b_top", [P, HEADS], F32)
        top_g, top_q = sb("b_top_g", [P, HEADS], F32), sb("b_top_q", [P, HEADS], F32)
        rz = sb("b_rz", [P, TK, 2, 2], F32)
        stats = sb("b_stats", [P, NT, 6], F32)
        mv = sb("b_mv", [P, NT, 2], F32)
        var_eps, half_neg = sb("b_var", [P, NT], F32), sb("b_half", [P, NT], F32)
        rstd, shift = sb("b_rstd", [P, NT], F32), sb("b_shift", [P, NT], F32)
        num = ctx_.enter_context(nc.psum_tensor("b_num", [P, 2, 2, IW], F32))
        den = ctx_.enter_context(nc.psum_tensor("b_den", [P, 2, IW], F32))
        pj = ctx_.enter_context(nc.psum_tensor("b_pj", [P, 2, IW], F32))

        weights_in = sem("b_weights_in")
        adj_in = [sem("b_adj_in0"), sem("b_adj_in1")]
        mask_built = sem("b_mask_built")
        mask_h_used = sem("b_mask_h_used")
        lone_ready = sem("b_lone_ready")
        const_ready = sem("b_const_ready")
        pool_step = sem("b_pool_step")
        wa_step = sem("b_wa_step")
        wx_ready = sem("b_wx_ready")
        x_in = sem("b_x_in")
        xr_in = [sem("b_xr_in0"), sem("b_xr_in1")]
        out_stored = [sem("b_out_stored0"), sem("b_out_stored1")]
        stats_made = sem("b_stats_made")
        waited = sem("b_waited")
        mv_ready = sem("b_mv_ready")
        rstd_ready = sem("b_rstd_ready")
        shift_ready = sem("b_shift_ready")
        h_ready = sem("b_h_ready")
        prep_ready = sem("b_prep_ready")
        prep_free = sem("b_prep_free")
        s_c_ready = sem("b_s_c_ready")
        dmax_ready = sem("b_dmax_ready")
        top_ready = sem("b_top_ready")
        tops_scaled = sem("b_tops_scaled")
        gq_ready = sem("b_gq_ready")
        q_taken = sem("b_q_taken")
        u_ready = [sem("b_u_ready0"), sem("b_u_ready1")]
        s_out = sem("b_s_out")
        s_in = [sem(f"b_s_in{i}") for i in range(HEADS)]
        relu_r = sem("b_relu_r")
        r_ready = sem("b_r_ready")
        p_ready = sem("b_p_ready")
        p_used = sem("b_p_used")
        sums_copied = sem("b_sums_copied")
        end_ready = sem("b_end_ready")
        end_free = sem("b_end_free")
        neg_ready = sem("b_neg_ready")
        neg_exp = sem("b_neg_exp")
        elu_step = sem("b_elu_step")
        out_ready = sem("b_out_ready")

        block = ctx_.enter_context(nc.Block())

        def groups_of(first, nxt):
            return [g for g in order if (nxt or g[0] == "end") and not (first and g[:2] == ("end", -1))]

        def bank_of(first, nxt):
            begin = G_PREP if first else G_PREP + len(groups_of(True, True))
            assert len(groups_of(False, True)) % 2 == 0
            return {g: (begin + i) % 2 for i, g in enumerate(groups_of(first, nxt))}

        def last_banks():
            used = G_PREP + len(groups_of(True, True)) + len(groups_of(False, False))
            return [(used + k) % 2 for k in range(G_END)]

        def batches(eng, batch):
            batch(0, True, True)
            with eng.Fori(1, B - 1) as b:
                batch(b, False, True)
            batch(B - 1, False, False)

        def stage(t):
            return p[:, t % 2, :, :].rearrange("p a n -> p (a n)").bitcast(I32)

        def stage_h(t):
            return p[:, 2 + t % 2, 0, :].bitcast(F16)

        def rows_of(dram, b):
            return dram[bass.ds(b, 1), :, :].rearrange("a (t p) f -> p (a t) f", p=P)

        def part_of(dram, b, n):
            rows = dram[bass.ds(b, 1), (n % 2) * HW:(n % 2 + 1) * HW, (n // 2) * P:(n // 2 + 1) * P]
            return rows.rearrange("a (t p) f -> p (a t) f", p=P)

        @block.sync
        def _(sp):
            sp.dma_start(hv[:], rows_of(x1, 0)).then_inc(x_in, 16)
            sp.dma_start(wx[:, :, 0:F], w.rearrange("(k p) n -> p k n", p=P)).then_inc(weights_in, 16)
            sp.dma_start(a_r[:], a.rearrange("(a n) -> a n", a=1).broadcast_to([P, 2 * D])).then_inc(weights_in, 16)
            for t in range(NT):
                if t >= 2:
                    sp.wait_ge(mask_built, 2 * (t - 1))
                sp.dma_start(stage(t), adjT[t * P:(t + 1) * P, :]).then_inc(adj_in[t % 2], 16)

            def rows_out(b):
                sp.wait_ge(prep_free, b * G_PREP + ROWS + 1)
                sp.sem_inc(waited, 1)
                sp.dma_start(s_dram, s_rows[:]).then_inc(s_out, 16)
                sp.wait_ge(s_out, 16 * b + 16)
                sp.sem_inc(waited, 1)

            def spread_s(b, heads):
                for hd in heads:
                    row = s_dram[hd * NT:(hd + 1) * NT, :].rearrange("(a t) p -> a (t p)", a=1)
                    sp.dma_start(r[:, hd, :], row.broadcast_to([P, N])).then_inc(s_in[hd], 16)

            def load_part(b, n, first):
                if not (first and n < 2):
                    sp.wait_ge(out_stored[n % 2], 16 * (2 * b + n // 2))
                    sp.sem_inc(waited, 1)
                sp.dma_start(xr[:, n % 2, :, :], part_of(x1, b, n)).then_inc(xr_in[n % 2], 16)

            def store_part(b, n):
                sp.wait_ge(out_ready, b * NH + n + 1)
                sp.sem_inc(waited, 1)
                sp.dma_start(part_of(out, b, n), xr[:, n % 2, :, :]).then_inc(out_stored[n % 2], 16)

            def batch(b, first, nxt):
                load_part(b, 0, first)
                if not first:
                    sp.wait_ge(p_ready, b * TB)
                    sp.sem_inc(waited, 1)
                spread_s(b, (2, 3))
                if nxt:
                    sp.wait_ge(u_ready[1], b + 1)
                    sp.sem_inc(waited, 1)
                    sp.dma_start(hv[:], rows_of(x1, b + 1)).then_inc(x_in, 16)
                if not first:
                    store_part(b - 1, 3)
                load_part(b, 1, first)
                store_part(b, 0)
                load_part(b, 2, first)
                store_part(b, 1)
                load_part(b, 3, first)
                if nxt:
                    for hd in (2, 3):
                        sp.wait_ge(s_in[hd], 16 * b + 16)
                        sp.sem_inc(waited, 1)
                    rows_out(b + 1)
                    sp.wait_ge(p_ready, b * TB + TB // 2)
                    sp.sem_inc(waited, 1)
                    spread_s(b + 1, (0, 1))
                store_part(b, 2)

            rows_out(0)
            spread_s(0, (0, 1))
            batches(sp, batch)
            store_part(B - 1, 3)
            for k in range(2):
                sp.wait_ge(out_stored[k], 16 * B * NH // 2)

        @block.gpsimd
        def _(pool):
            pool.memset(ident[:], 0.0).then_inc(pool_step, 1)
            pool.memset(half_neg[:], -0.5).then_inc(pool_step, 1)
            pool.memset(ones[:], 1.0).then_inc(const_ready, 1)
            pool.memset(ones_h[:], 1.0).then_inc(const_ready, 1)
            pool.wait_ge(pool_step, 2)
            pool.affine_select(out=ident[:], in_=ident[:], compare_op=ALU.not_equal, fill=1.0, base=0,
                               pattern=[[-1, P]], channel_multiplier=1).then_inc(const_ready, 1)
            with pool.Fori(0, B) as b:
                pool.wait_ge(mv_ready, b + 1)
                pool.sem_inc(waited, 1)
                nc.gpsimd.tensor_scalar(var_eps[:], mv[:, :, 1], EPS, None, ALU.add).then_inc(pool_step, 1)
                pool.wait_ge(pool_step, b + 3)
                nc.gpsimd.tensor_tensor(rstd[:], var_eps[:], half_neg[:], ALU.pow).then_inc(rstd_ready, 1)
                pool.wait_ge(dmax_ready, b + 1)
                pool.sem_inc(waited, 1)
                nc.gpsimd.partition_all_reduce(top[:], dmax[:], P, RMAX).then_inc(top_ready, 1)

        @block.scalar
        def _(act):
            nc.scalar.preload_act_table_set("natural_log_exp_and_others")

            def make_h(b):
                act.wait_ge(shift_ready, b + 1)
                for t in range(NT):
                    nc.scalar.activation(hv[:, t, :], hv[:, t, :], ACT.Relu, bias=shift[:, t:t + 1],
                                         scale=rstd[:, t:t + 1]).then_inc(h_ready, 1)

            def move_group(b, k, bank):
                act.wait_ge(prep_ready, b * G_PREP + k + 1)
                if k < G_TR:
                    nc.scalar.activation(hT[:, k % KT, (k // KT) * IW:(k // KT + 1) * IW], pj[:, bank, :],
                                         ACT.Copy).then_inc(prep_free, 1)
                elif k < G_TR + G_PJ:
                    nc.scalar.activation(hv[:, k - G_TR, :], pj[:, bank, 0:F], ACT.Copy)
                    nc.scalar.activation(sd[:, k - G_TR, :], pj[:, bank, F:FX], ACT.Copy).then_inc(prep_free, 1)
                elif k == ROWS:
                    nc.scalar.activation(s_rows[:], pj[0:HEADS * NT, bank, 0:P], ACT.Copy).then_inc(prep_free, 1)
                else:
                    nc.scalar.activation(mean_v[:], pj[0:1, bank, 0:F], ACT.Copy, scale=1.0 / N).then_inc(prep_free, 1)

            def make_gq(b):
                act.wait_ge(tops_scaled, b + 1)
                for hd in range(HEADS):
                    d = sd[:, :, HEADS + hd]
                    nc.scalar.activation(g[:, hd, :], d, ACT.Exp, bias=top_g[:, hd:hd + 1], scale=ALPHA)
                    last = nc.scalar.activation(q_next[:, hd, :], d, ACT.Exp, bias=top_q[:, hd:hd + 1],
                                                scale=1.0 - ALPHA)
                last.then_inc(gq_ready, 1)

            def make_r(b, heads):
                for hd in heads:
                    act.wait_ge(s_in[hd], 16 * b + 16)
                    nc.scalar.activation(r[:, hd, :], r[:, hd, :], ACT.Relu, bias=top[:, hd:hd + 1]).then_inc(relu_r, 1)
                    act.wait_ge(relu_r, b * HEADS + hd + 1)
                    nc.scalar.activation(r[:, hd, :], r[:, hd, :], ACT.Exp, scale=ALPHA - 1.0).then_inc(r_ready, 1)

            def copy_sums(b, n):
                act.wait_ge(p_used, PB + (b * NH + n + 1) * NT)
                nc.scalar.activation(den_s[:, n % 2, :], den[:, n % 2, :], ACT.Copy).then_inc(sums_copied, 1)
                nc.scalar.activation(num_s[:, n % 2, :, :], num[:, n % 2, :, :], ACT.Copy).then_inc(sums_copied, 1)

            def exp_neg(b, n):
                act.wait_ge(neg_ready, b * NH + n + 1)
                nc.scalar.activation(neg[:], neg[:], ACT.Exp).then_inc(neg_exp, 1)

            def batch(b, first, nxt):
                at = bank_of(first, nxt)

                def move(k0, k1):
                    if nxt:
                        for k in range(k0, k1):
                            move_group(b + 1, k, at[("prep", k)])

                if not first:
                    copy_sums(b - 1, 3)
                make_r(b, (2, 3))
                if not first:
                    exp_neg(b - 1, 3)
                copy_sums(b, 0)
                exp_neg(b, 0)
                if nxt:
                    make_h(b + 1)
                copy_sums(b, 1)
                move(0, 6)
                exp_neg(b, 1)
                move(6, G_TR + G_PJ)
                copy_sums(b, 2)
                move(ROWS, ROWS + 1)
                if nxt:
                    make_gq(b + 1)
                    move(MEAN, MEAN + 1)
                exp_neg(b, 2)
                if nxt:
                    make_r(b + 1, (0, 1))

            make_h(0)
            for k in range(G_PREP):
                move_group(0, k, k % 2)
            make_gq(0)
            make_r(0, (0, 1))
            batches(act, batch)
            copy_sums(B - 1, 3)
            exp_neg(B - 1, 3)

        @block.vector
        def _(dve):
            def stats_of(t):
                nc.vector.bn_stats(stats[:, t, :], hv[:, t, :]).then_inc(stats_made, 1)

            def aggregate(b):
                dve.wait_ge(stats_made, (b + 1) * NT)
                dve.sem_inc(waited, 1)
                for t in range(NT):
                    last = nc.vector.bn_aggr(mv[:, t, :], stats[:, t, :])
                last.then_inc(mv_ready, 1)

            def make_shift(b):
                dve.wait_ge(rstd_ready, b + 1)
                nc.vector.scalar_tensor_tensor(shift[:], mv[:, :, 0], -1.0, rstd[:], ALU.mult,
                                               ALU.mult).then_inc(shift_ready, 1)

            def take_s(b):
                dve.wait_ge(prep_free, b * G_PREP + G_TR + G_PJ)
                nc.vector.tensor_copy(s_c[:].rearrange("p h t -> p t h"), sd[:, :, 0:HEADS]).then_inc(s_c_ready, 1)
                nc.vector.reduce_max(dmax[:], sd[:, :, HEADS:].rearrange("p t h -> p h t"),
                                     axis=AX_X).then_inc(dmax_ready, 1)

            def scale_top(b):
                dve.wait_ge(top_ready, b + 1)
                nc.vector.tensor_scalar(top_g[:], top[:], -ALPHA, None, ALU.mult)
                nc.vector.tensor_scalar(top_q[:], top[:], ALPHA - 1.0, None, ALU.mult).then_inc(tops_scaled, 1)

            def make_u(b, hd):
                dve.wait_ge(gq_ready, b + 1)
                cols = slice(hd * D, (hd + 1) * D)
                gain = g[:, hd, :].rearrange("p (t z) -> p t z", z=1)
                nc.vector.tensor_tensor(u[:, :, cols], hv[:, :, cols], gain.broadcast_to([P, NT, D]), ALU.mult)
                last = nc.vector.tensor_copy(g32[:, :, hd, :], gain.broadcast_to([P, NT, 32]))
                if hd % 2:
                    last.then_inc(u_ready[hd // 2], 1)

            def weigh(b, n, jt):
                dve.wait_ge(p_used, b * TB + n * NT + jt + 1)
                cols = slice((n % 2) * HW, (n % 2 + 1) * HW)
                for k in range(2):
                    hd = 2 * (n // 2) + k
                    last = nc.vector.scalar_tensor_tensor(p[:, jt % PB, k, :], r[:, hd, cols], q[:, hd, jt:jt + 1],
                                                          mask[:, jt, cols], ALU.max, ALU.mult)
                last.then_inc(p_ready, 1)

            def finish_sums(b, n, banks):
                m = b * NH + n
                dve.wait_ge(end_ready, m * G_END + 1)
                sums = pj[:, banks[0], :].rearrange("p (k c z) -> p k c z", k=TK, c=4)[:, :, :, 0]
                nc.vector.reciprocal(rz[:].rearrange("p k a c -> p k (a c)"), sums).then_inc(end_free, 1)
                dve.wait_ge(end_free, m * G_END + 1)
                for ib in range(2):
                    dve.wait_ge(end_ready, m * G_END + 2 + ib)
                    scale = rz[:, :, :, ib].rearrange("p k (a z) -> p k a z", z=1).broadcast_to([P, TK, 2, D])
                    nc.vector.tensor_tensor(y[:, ib * TK:(ib + 1) * TK, :].rearrange("p k (a d) -> p k a d", a=2),
                                            pj[:, banks[1 + ib], :].rearrange("p (k a d) -> p k a d", k=TK, a=2),
                                            scale, ALU.mult).then_inc(end_free, 1)
                dve.wait_ge(end_free, (m + 1) * G_END)
                nc.vector.tensor_scalar(neg[:], y[:], 0.0, None, ALU.min).then_inc(neg_ready, 1)

            def finish_elu(b, n):
                m = b * NH + n
                dve.wait_ge(neg_exp, m + 1)
                nc.vector.scalar_tensor_tensor(y[:], y[:], 0.0, neg[:], ALU.max, ALU.add).then_inc(elu_step, 1)
                dve.wait_ge(xr_in[n % 2], 16 * (2 * b + n // 2) + 16)
                dve.wait_ge(elu_step, m + 1)
                part = xr[:, n % 2, :, :]
                nc.vector.scalar_tensor_tensor(part, y[:], -1.0, part, ALU.add, ALU.add).then_inc(out_ready, 1)

            def batch(b, first, nxt):
                at = bank_of(first, nxt)
                if not first:
                    dve.wait_ge(p_ready, b * TB)
                nc.vector.tensor_copy(q[:], q_next[:]).then_inc(q_taken, 1)
                dve.wait_ge(q_taken, b + 1)
                for n in range(NH):
                    if n % 2 == 0:
                        dve.wait_ge(r_ready, b * HEADS + n + 2)
                    for jt in range(NT):
                        weigh(b, n, jt)
                        i = n * NT + jt
                        if i in (4, 5):
                            make_u(b, i - 2)
                        if jt == 6 and not (first and n == 0):
                            bb, nn = (b, n - 1) if n else (b - 1, 3)
                            finish_sums(bb, nn, [at[("end", n - 1, k)] for k in range(G_END)])
                        if jt == 9 and not (first and n == 0):
                            finish_elu(*((b, n - 1) if n else (b - 1, 3)))
                        if nxt:
                            if 10 <= i < 10 + NT:
                                if i == 10:
                                    dve.wait_ge(x_in, 16 * b + 32)
                                stats_of(i - 10)
                            if i == 26:
                                aggregate(b + 1)
                            if i == 28:
                                make_shift(b + 1)
                            if i == 49:
                                take_s(b + 1)
                            if i == 50:
                                scale_top(b + 1)
                            if i in (52, 53):
                                make_u(b + 1, i - 52)

            dve.wait_ge(x_in, 16)
            for t in range(NT):
                stats_of(t)
            aggregate(0)
            make_shift(0)
            dve.wait_ge(weights_in, 32)
            n = 0
            for kt in range(KT):
                for part in range(2):
                    if n:
                        dve.wait_ge(wa_step, 2 * n)
                    nc.vector.tensor_tensor(wa[:], wx[:, kt, 0:F].rearrange("p (h d) -> p h d", h=HEADS),
                                            spread(a_r[:, part * D:(part + 1) * D], HEADS), ALU.mult).then_inc(wa_step, 1)
                    dve.wait_ge(wa_step, 2 * n + 1)
                    nc.vector.reduce_sum(wx[:, kt, F + part * HEADS:F + (part + 1) * HEADS], wa[:],
                                         axis=AX_X).then_inc(wa_step, 1)
                    n += 1
            dve.wait_ge(wa_step, 2 * n)
            dve.sem_inc(wx_ready, 1)
            dve.wait_ge(const_ready, 2)
            for t in range(NT):
                dve.wait_ge(adj_in[t % 2], 16 * (t // 2 + 1))
                nc.vector.tensor_scalar(mask[:, t, :], stage(t), 0.0, None, ALU.is_gt).then_inc(mask_built, 1)
                if t >= 2:
                    dve.wait_ge(mask_h_used, t - 1)
                nc.vector.tensor_scalar(stage_h(t), stage(t), 0.0, None, ALU.is_gt).then_inc(mask_built, 1)
            dve.wait_ge(mask_h_used, NT)
            nc.vector.tensor_scalar(lone[:], num[0:1, :, :, :].rearrange("p a b n -> p (a b n)"), 0.0, None,
                                    ALU.is_equal).then_inc(lone_ready, 1)
            take_s(0)
            scale_top(0)
            make_u(0, 0)
            make_u(0, 1)
            batches(dve, batch)
            finish_sums(B - 1, 3, last_banks())
            finish_elu(B - 1, 3)

        @block.tensor
        def _(pe):
            def prepare(b, k, bank):
                if k < G_TR:
                    pe.wait_ge(h_ready, b * NT + 4 * (k // KT) + 4)
                    for i in range(4):
                        t = 4 * (k // KT) + i
                        last = nc.tensor.transpose(pj[:, bank, i * P:(i + 1) * P],
                                                   hv[:, t, (k % KT) * P:(k % KT + 1) * P], ident[:])
                elif k < G_TR + G_PJ:
                    t = k - G_TR
                    if t == 0:
                        pe.wait_ge(prep_free, b * G_PREP + G_TR)
                    for kt in range(KT):
                        last = nc.tensor.matmul(pj[:, bank, 0:FX], hT[:, kt, t * P:(t + 1) * P], wx[:, kt, :],
                                                start=(kt == 0), stop=(kt == KT - 1))
                elif k == ROWS:
                    pe.wait_ge(s_c_ready, b + 1)
                    pe.sem_inc(waited, 1)
                    last = nc.tensor.transpose(pj[0:HEADS * NT, bank, 0:P], s_c[:].rearrange("p h t -> p (h t)"),
                                               ident[:])
                else:
                    for t in range(NT):
                        last = nc.tensor.matmul(pj[0:1, bank, 0:F], ones[:, 0:1], hv[:, t, :],
                                                start=(t == 0), stop=(t == NT - 1))
                last.then_inc(prep_ready, 1)

            def finish(b, n, k, bank):
                pe.wait_ge(sums_copied, 2 * (b * NH + n) + min(k, 1) + 1)
                src = den_s[:, n % 2, :] if k == 0 else num_s[:, n % 2, k - 1, :]
                for i in range(TK):
                    last = nc.tensor.transpose(pj[:, bank, i * P:(i + 1) * P], src[:, i * P:(i + 1) * P], ident[:])
                last.then_inc(end_ready, 1)

            def released(b, group):
                if group[0] == "prep":
                    return prep_free, (b + 1) * G_PREP + group[1] + 1
                return end_free, (b * NH + group[1]) * G_END + group[2] + 1

            def batch(b, first, nxt):
                groups, at = groups_of(first, nxt), bank_of(first, nxt)
                if first:
                    before = [(prep_free, ROWS + 1), (prep_free, MEAN + 1)]
                else:
                    before = [released(b - 1, g_) for g_ in order[-2:]]
                frees = before + [released(b, g_) for g_ in groups]
                done = 0
                for n in range(NH):
                    s, pr = n % 2, n // 2
                    m = b * NH + n
                    rows = (n % 2) * HW
                    if not (first and n < 2):
                        pe.wait_ge(sums_copied, 2 * (m - 1))
                    if n % 2 == 0:
                        if n == 0:
                            pe.wait_ge(prep_free, (b + 1) * G_PREP)
                        pe.wait_ge(u_ready[pr], b + 1)
                    for ib in range(2):
                        alone = lone[0:1, rows + ib * IW:rows + (ib + 1) * IW]
                        for k in range(2):
                            nc.tensor.matmul(num[k * D:(k + 1) * D, s, ib, :],
                                             mean_v[0:1, pr * P + k * D:pr * P + (k + 1) * D], alone,
                                             start=True, stop=False)
                    for ib in range(2):
                        alone = lone[0:1, rows + ib * IW:rows + (ib + 1) * IW]
                        for k in range(2):
                            c = 2 * k + ib
                            nc.tensor.matmul(den[c * 32:(c + 1) * 32, s, :], ones[0:1, :], alone,
                                             start=True, stop=False)
                    for jt in range(NT):
                        end = jt == NT - 1
                        pe.wait_ge(p_ready, b * TB + n * NT + jt + 1)
                        for ib in range(2):
                            for k in range(2):
                                nc.tensor.matmul(num[k * D:(k + 1) * D, s, ib, :],
                                                 u[:, jt, pr * P + k * D:pr * P + (k + 1) * D],
                                                 p[:, jt % PB, k, ib * IW:(ib + 1) * IW], start=False, stop=end)
                        for ib in range(2):
                            for k in range(2):
                                c = 2 * k + ib
                                last = nc.tensor.matmul(den[c * 32:(c + 1) * 32, s, :], g32[:, jt, 2 * pr + k, :],
                                                        p[:, jt % PB, k, ib * IW:(ib + 1) * IW],
                                                        start=False, stop=end)
                        last.then_inc(p_used, 1)
                        for g_ in behind[n * NT + jt]:
                            if g_ not in at:
                                continue
                            pe.wait_ge(*frees[done])
                            done += 1
                            if g_[0] == "prep":
                                prepare(b + 1, g_[1], at[g_])
                            else:
                                bb, nn = (b, g_[1]) if g_[1] >= 0 else (b - 1, 3)
                                finish(bb, nn, g_[2], at[g_])

            pe.wait_ge(const_ready, 3)
            for k in range(G_TR):
                if k >= 2:
                    pe.wait_ge(prep_free, k - 1)
                prepare(0, k, k % 2)
            for t in range(NT):
                pe.wait_ge(mask_built, 2 * t + 2)
                for k in range(N // IW):
                    last = nc.tensor.matmul(num[0:1, k // 2, k % 2, :], ones_h[:], stage_h(t)[:, k * IW:(k + 1) * IW],
                                            start=(t == 0), stop=(t == NT - 1))
                last.then_inc(mask_h_used, 1)
                if t == 0:
                    pe.wait_ge(wx_ready, 1)
                pe.wait_ge(prep_free, G_TR + t - 1)
                prepare(0, G_TR + t, (G_TR + t) % 2)
            for k in (ROWS, MEAN):
                pe.wait_ge(prep_free, k - 1)
                prepare(0, k, k % 2)
            pe.wait_ge(lone_ready, 1)
            pe.sem_inc(p_used, PB)
            batches(pe, batch)
            for k in range(G_END):
                if k == 0:
                    pe.wait_ge(end_free, (B * NH - 1) * G_END)
                if k == 2:
                    pe.wait_ge(end_free, (B * NH - 1) * G_END + 1)
                finish(B - 1, 3, k, last_banks()[k])


def kernel(**inputs):
    import numpy as _np
    import concourse.bacc as _bacc
    from concourse import mybir as _mybir
    from concourse.bass_utils import run_bass_kernel_spmd as _run

    nc = _bacc.Bacc("TRN2", target_bir_lowering=False, num_devices=1)
    arrays = {}

    def put(name, a):
        a = _np.ascontiguousarray(a)
        arrays[name] = a
        return nc.dram_tensor(name, a.shape, _mybir.dt.from_np(a.dtype), kind="ExternalInput").ap()

    x = _np.asarray(inputs["x"])
    B, N, F = x.shape
    f32 = _mybir.dt.float32
    x_d = put("x", x)
    adjT = put("adjT", _np.asarray(inputs["adj"]).T)
    wT = {k: put(f"w{k}T", _np.asarray(inputs[f"L0_gnn_W{k}"]).T) for k in "qkvo"}
    bc = {k: put(f"b{k}", _np.asarray(inputs[f"L0_gnn_b{k}"]).reshape(F // P, P).T) for k in "qk"}
    br = {k: put(f"b{k}", inputs[f"L0_gnn_b{k}"]) for k in "vo"}
    gamma, beta = put("gamma", inputs["L0_gnn_gamma"]), put("beta", inputs["L0_gnn_beta"])
    w1, a1 = put("w1", inputs["L1_gnn_W"]), put("a1", inputs["L1_gnn_a"])
    x1 = nc.dram_tensor("x1", (B, N, F), f32, kind="Internal").ap()
    s_rows = nc.dram_tensor("s_rows", (4 * N // P, P), f32, kind="Internal").ap()
    out = nc.dram_tensor("out", (B, N, F), f32, kind="ExternalOutput").ap()
    layer0(nc, x_d, adjT, wT["q"], bc["q"], wT["k"], bc["k"], wT["v"], br["v"], wT["o"], br["o"], gamma, beta, x1)
    layer1(nc, x1, adjT, w1, a1, s_rows, out)
    r = _run(nc, [arrays], core_ids=[0])
    return r.results[0]["out"]
```

```python
import math

import concourse.bass as bass
from concourse import mybir
from contextlib import ExitStack

ALU = mybir.AluOpType
ACT = mybir.ActivationFunctionType
AX_X = mybir.AxisListType.X
F32 = mybir.dt.float32
F16 = mybir.dt.float16
I32 = mybir.dt.int32
U8 = mybir.dt.uint8
RMAX = bass.bass_isa.ReduceOp.max

P = 128
IW = 512
CHUNK = 256
CLIP = 10.0
EPS = 1e-5
ALPHA = 0.2
BEHIND = 2
LAG = 2
EBUF = 8


def spread(ap, n):
    p, m = ap.shape
    return ap.rearrange("p (a m) -> p a m", a=1).broadcast_to([p, n, m])


def layer0(nc, x, adjT, wqT, bq, wkT, bk, wvT, bv, bv_cols, woT, bo, gamma, beta, near, x1):
    B, N, F = x.shape
    NT = N // P
    KT = F // P
    D = F // 4
    PAIRS = F // (2 * D)
    IB = N // IW
    NCH = N // CHUNK
    JC = CHUNK // P
    assert PAIRS == KT == 2 and 2 * D == P and JC == 2 and NT % EBUF == 0
    X_IN = 4
    STAGES = 6
    NEAR = NT // 2
    LO, HI = math.exp(-CLIP), math.exp(CLIP)

    G_TR, G_V, G_QK, G_WO = KT * NT // 4, NT // 2, 2 * IB, NT // 2
    G_FIRST = G_TR + G_QK + G_V
    G_B = G_QK + G_QK + G_V
    J_B = G_WO + G_TR
    T_IB, T_PR, T_B = NT, IB * NT, PAIRS * IB * NT
    C_IB, C_PR, C_B = NCH, IB * NCH, PAIRS * IB * NCH
    CUT_FIRST, CUT_OTHER = (set(), {1, 3, 5, 7, 9, 11, 13}), {3, 7, 11}
    ADD_FIRST, ADD_OTHER = ({NCH - 1}, {NCH - 1}), set(range(NCH)) - {1, 3, 5}
    assert all(NT - 1 not in s for s in (*CUT_FIRST, CUT_OTHER))
    assert all(NCH - 1 in s for s in (*ADD_FIRST, ADD_OTHER)) and BEHIND <= JC

    def cuts_of(pr, ib):
        return CUT_FIRST[pr] if isinstance(ib, int) and ib == 0 else CUT_OTHER

    def adds_of(pr, ib):
        return ADD_FIRST[pr] if isinstance(ib, int) and ib == 0 else ADD_OTHER

    def count(b, pr, ib, first, other, upto):
        pair = [len(first[k]) + (IB - 1) * len(other) for k in range(PAIRS)]
        base = b * sum(pair) + sum(pair[:pr])
        if isinstance(ib, int) and ib == 0:
            return base + len([t for t in first[pr] if t <= upto])
        before = ib * len(other) + len([t for t in other if t <= upto])
        more = len(first[pr]) - len(other)
        return base + before + more

    def cuts(b, pr, ib, jt):
        return count(b, pr, ib, CUT_FIRST, CUT_OTHER, jt)

    def cuts_scalar(b, pr, ib, jt):
        return count(b, pr, ib, [set(range(NT)) - s for s in CUT_FIRST], set(range(NT)) - CUT_OTHER, jt)

    def adds(b, pr, ib, c):
        return count(b, pr, ib, ADD_FIRST, ADD_OTHER, c)

    S_K, S_Q = 8 * 16, 4 * 16

    with ExitStack() as ctx_:
        def sb(name, shape, dt):
            return ctx_.enter_context(nc.sbuf_tensor(name, shape, dt))

        def sem(name):
            return ctx_.enter_context(nc.semaphore(name))

        mask = sb("a_mask", [P, NT, N], U8)
        h = sb("a_h", [P, NT, F], F32)
        xr = sb("a_xr", [P, NT, F], F32)
        o = sb("a_o", [P, NT, F], F32)
        hT = sb("a_hT", [P, KT, N], F32)
        v = sb("a_v", [P, NT, F], F32)
        ctxT = sb("a_ctxT", [P, PAIRS, N], F32)
        q_st = sb("a_q_st", [P, 2, N], F16)
        kh_st = sb("a_kh_st", [P, 2, N], F16)
        kl_st = sb("a_kl_st", [P, 2, N], F16)
        e = sb("a_e", [P, EBUF, 2, IW], F32)
        k_hi, k_lo, q_hi, q_lo = (e[:, i, :, :].rearrange("p a n -> p (a n)").bitcast(F16) for i in range(2, 6))
        wq, wk = sb("a_wq", [P, KT, F], F32), sb("a_wk", [P, KT, F], F32)
        wv, wo = sb("a_wv", [P, KT, F], F32), sb("a_wo", [P, KT, F], F32)
        bq_c, bk_c = sb("a_bq", [P, PAIRS], F32), sb("a_bk", [P, PAIRS], F32)
        bv_r, bo_r = sb("a_bv", [P, F], F32), sb("a_bo", [P, F], F32)
        gamma_r, beta_r = sb("a_gamma", [P, F], F32), sb("a_beta", [P, F], F32)
        both = sb("a_both", [P, 2, 2, IW], F32)
        h_sum = sb("a_h_sum", [P, KT, NCH], F32)
        v_sum = sb("a_v_sum", [P, PAIRS, NCH], F32)
        bv_c, bv_lo = sb("a_bv_c", [P, PAIRS], F32), sb("a_bv_lo", [P, PAIRS], F32)
        consts = sb("a_consts", [P, 3], F32)
        minus_lo, lo_sum, half_neg = (consts[:, i:i + 1] for i in range(3))
        part = sb("a_part", [P, IW], F32)
        ident = sb("a_ident", [P, P], F32)
        ones = sb("a_ones", [P, D], F32)
        stats = sb("a_stats", [P, NT, 6], F32)
        mv = sb("a_mv", [P, NT, 2], F32)
        rstd_x, shift_x = sb("a_rstd_x", [P, NT], F32), sb("a_shift_x", [P, NT], F32)
        rstd_r, shift_r = sb("a_rstd_r", [P, NT], F32), sb("a_shift_r", [P, NT], F32)
        rstd_o = sb("a_rstd_o", [P, NT], F32)
        sc = ctx_.enter_context(nc.psum_tensor("a_sc", [P, 4, IW], F32))
        num = ctx_.enter_context(nc.psum_tensor("a_num", [P, 2, IW], F32))
        den = ctx_.enter_context(nc.psum_tensor("a_den", [P, IW], F32))
        pj = ctx_.enter_context(nc.psum_tensor("a_pj", [P, IW], F32))

        weights_in = sem("a_weights_in")
        adj_in = [sem(f"a_adj_in{k}") for k in range(STAGES)]
        mask_built = sem("a_mask_built")
        near_stored = [sem(f"a_near_stored{k}") for k in range(NEAR)]
        const_ready = sem("a_const_ready")
        x_begun = [sem(f"a_x_begun{k}") for k in range(X_IN)]
        last_ready = sem("a_last_ready")
        last_stored = sem("a_last_stored")
        x_in = sem("a_x_in")
        xr_in = sem("a_xr_in")
        x1_stored = sem("a_x1_stored")
        stats_made = sem("a_stats_made")
        waited = sem("a_waited")
        mv_ready = sem("a_mv_ready")
        pool_step = sem("a_pool_step")
        rstd_ready = sem("a_rstd_ready")
        shift_ready = sem("a_shift_ready")
        kept = sem("a_kept")
        h_ready = sem("a_h_ready")
        o_ready = sem("a_o_ready")
        bias_added = sem("a_bias_added")
        group_ready = sem("a_group_ready")
        group_free = sem("a_group_free")
        behind_ready = sem("a_behind_ready")
        behind_free = sem("a_behind_free")
        hi_ready = sem("a_hi_ready")
        k_stacked, q_stacked = sem("a_k_stacked"), sem("a_q_stacked")
        k_begun, q_begun = sem("a_k_begun"), sem("a_q_begun")
        scores_ready = sem("a_scores_ready")
        exp_ready = sem("a_exp_ready")
        cut = sem("a_cut")
        cut_here = sem("a_cut_here")
        p_ready = sem("a_p_ready")
        both_ready = sem("a_both_ready")
        den_made = sem("a_den_made")
        h_summed = sem("a_h_summed")
        v_sum_ready = sem("a_v_sum_ready")
        v_sum_made = sem("a_v_sum_made")
        bv_scaled = sem("a_bv_scaled")
        p_used = sem("a_p_used")
        ln_ready = sem("a_ln_ready")
        inverse_ready = sem("a_inverse_ready")
        chunk_free = sem("a_chunk_free")
        ctx_added = sem("a_ctx_added")
        ctx_done = sem("a_ctx_done")
        post_step = sem("a_post_step")
        out_ready = sem("a_out_ready")

        block = ctx_.enter_context(nc.Block())

        def stage(t):
            k, half = (t % STAGES) // 2, t % 2
            if k == 0:
                return e[:, 6 * half:6 * half + 2, :, :].rearrange("p a b n -> p (a b n)").bitcast(I32)
            if k == 1:
                return ctxT[:, half, :].bitcast(I32)
            return o[:, half * NT // 2:(half + 1) * NT // 2, :].rearrange("p t f -> p (t f)").bitcast(I32)

        def near_tile(t):
            return v[:, (t % NEAR) * 2:(t % NEAR) * 2 + 2, :].rearrange("p a f -> p (a f)").bitcast(U8)[:, 0:N]

        def rows_of(dram, b):
            return dram[bass.ds(b, 1), :, :].rearrange("a (t p) f -> p (a t) f", p=P)

        def g_qk1(b):
            return b * G_B + G_FIRST

        def g_qk_next(b):
            return b * G_B + G_FIRST + G_QK

        def g_v_next(b):
            return b * G_B + G_FIRST + G_QK + G_QK

        def j_wo(b):
            return b * J_B - G_WO

        def j_tr(b, first):
            return 0 if first else b * J_B

        @block.sync
        def _(sp):
            for k in range(X_IN):
                tiles = slice(k * NT // X_IN, (k + 1) * NT // X_IN)
                sp.dma_start(h[:, tiles, :], rows_of(x, 0)[:, tiles, :]).then_inc(x_begun[k], 16)
            for w, src in ((wq, wqT), (wk, wkT), (wv, wvT), (wo, woT)):
                sp.dma_start(w[:], src.rearrange("(k p) n -> p k n", p=P)).then_inc(weights_in, 16)
            for c, src in ((bq_c, bq), (bk_c, bk), (bv_c, bv_cols)):
                sp.dma_start(c[:], src).then_inc(weights_in, 16)
            for r, src in ((bv_r, bv), (bo_r, bo), (gamma_r, gamma), (beta_r, beta)):
                sp.dma_start(r[:], src.rearrange("(a n) -> a n", a=1).broadcast_to([P, F])).then_inc(weights_in, 16)
            def store_near(t):
                sp.wait_ge(mask_built, 2 * (t + 1))
                sp.dma_start(near[t * P:(t + 1) * P, :], near_tile(t)).then_inc(near_stored[t % NEAR], 16)

            for t in range(NT):
                if t >= STAGES:
                    store_near(t - STAGES)
                sp.dma_start(stage(t), adjT[t * P:(t + 1) * P, :]).then_inc(adj_in[t % STAGES], 16)
            for t in range(NT - STAGES, NT):
                store_near(t)

            def stack(g):
                def stack_k(cols, groups, done):
                    sp.wait_ge(group_free, g + 4 + groups)
                    for hd in range(2):
                        mine = slice(hd * D, (hd + 1) * D)
                        for dst, src in ((kh_st, k_hi), (kl_st, k_lo)):
                            sp.dma_start(dst[0:D, hd, cols], src[mine, cols]).then_inc(done, 16)
                            sp.dma_start(dst[D:P, hd, cols], src[mine, cols]).then_inc(done, 16)

                def stack_q(cols, groups, done):
                    sp.wait_ge(group_free, g + 4 + IB + groups)
                    for hd in range(2):
                        mine = slice(hd * D, (hd + 1) * D)
                        sp.dma_start(q_st[0:D, hd, cols], q_hi[mine, cols]).then_inc(done, 16)
                        sp.dma_start(q_st[D:P, hd, cols], q_lo[mine, cols]).then_inc(done, 16)

                stack_k(slice(0, N // 2), IB // 2, k_begun)
                stack_q(slice(0, IW), 1, q_begun)
                stack_k(slice(N // 2, N), IB, k_stacked)
                stack_q(slice(IW, N), IB, q_stacked)

            def store(b):
                sp.wait_ge(out_ready, b + 1)
                sp.sem_inc(waited, 1)
                sp.dma_start(rows_of(x1, b), o[:]).then_inc(x1_stored, 16)

            def batch(b, first, nxt):
                if nxt:
                    if first:
                        sp.wait_ge(group_free, G_TR + 4)
                    else:
                        sp.wait_ge(behind_free, j_wo(b) + 1)
                        sp.sem_inc(waited, 1)
                    sp.dma_start(h[:], rows_of(x, b + 1)).then_inc(x_in, 16)
                if not first:
                    store(b - 1)
                sp.dma_start(xr[:], rows_of(x, b)).then_inc(xr_in, 16)
                stack(g_qk1(b))
                if nxt:
                    stack(g_qk_next(b))

            sp.sem_inc(x1_stored, 16)
            stack(G_TR)
            batch(0, True, True)
            with sp.Fori(1, B - 1) as b:
                batch(b, False, True)
            batch(B - 1, False, False)
            for k in range(X_IN):
                tiles = slice(k * NT // X_IN, (k + 1) * NT // X_IN)
                sp.wait_ge(last_ready, k + 1)
                sp.dma_start(rows_of(x1, B - 1)[:, tiles, :], o[:, tiles, :]).then_inc(last_stored, 16)
            sp.wait_ge(x1_stored, 16 * B)
            sp.wait_ge(last_stored, 16 * X_IN)

        @block.gpsimd
        def _(pool):
            pool.memset(ident[:], 0.0).then_inc(pool_step, 1)
            pool.memset(ones[:], 1.0).then_inc(const_ready, 1)
            pool.memset(minus_lo, -LO).then_inc(const_ready, 1)
            pool.memset(lo_sum, CHUNK * LO).then_inc(const_ready, 1)
            pool.memset(half_neg, -0.5).then_inc(pool_step, 1)
            pool.wait_ge(pool_step, 2)
            pool.affine_select(out=ident[:], in_=ident[:], compare_op=ALU.not_equal, fill=1.0, base=0,
                               pattern=[[-1, P]], channel_multiplier=1).then_inc(const_ready, 1)
            pool.wait_ge(weights_in, 176)

            def make_rstd(k, rstd):
                pool.wait_ge(mv_ready, k + 1)
                pool.sem_inc(waited, 1)
                nc.gpsimd.tensor_scalar(rstd[:], mv[:, :, 1], EPS, None, ALU.add).then_inc(pool_step, 1)
                pool.wait_ge(pool_step, k + 3)
                nc.gpsimd.tensor_tensor(rstd[:], rstd[:], half_neg.broadcast_to([P, NT]), ALU.pow).then_inc(rstd_ready, 1)

            def batch(b, first, nxt):
                if not first:
                    make_rstd(2 * b, rstd_o)
                if nxt:
                    make_rstd(2 * b + 1, rstd_x)
                pool.wait_ge(o_ready, (b + 1) * NT)
                nc.gpsimd.tensor_tensor(o[:], o[:], spread(bo_r[:], NT), ALU.add).then_inc(bias_added, 1)
                nc.gpsimd.tensor_tensor(xr[:], xr[:], spread(beta_r[:], NT), ALU.add).then_inc(bias_added, 1)

            make_rstd(0, rstd_x)
            batch(0, True, True)
            with pool.Fori(1, B - 1) as b:
                batch(b, False, True)
            batch(B - 1, False, False)
            make_rstd(2 * B - 1, rstd_o)

        @block.scalar
        def _(act):
            nc.scalar.preload_act_table_set("natural_log_exp_and_others")
            act.sem_inc(ln_ready, 1)

            def make_h(t):
                nc.scalar.activation(h[:, t, :], h[:, t, :], ACT.Relu, bias=shift_x[:, t:t + 1],
                                     scale=rstd_x[:, t:t + 1]).then_inc(h_ready, 1)

            def make_o(t):
                nc.scalar.activation(o[:, t, :], xr[:, t, :], ACT.Relu, bias=shift_r[:, t:t + 1],
                                     scale=rstd_r[:, t:t + 1]).then_inc(o_ready, 1)

            def high_halves(first, pr, groups):
                for g in groups:
                    to, bias = ((k_hi, bk_c), (q_hi, bq_c))[g // IB]
                    act.wait_ge(group_ready, first + g + 1)
                    nc.scalar.activation(to[:, (g % IB) * IW:(g % IB + 1) * IW], sc[:, g % 4, :], ACT.Identity,
                                         bias=bias[:, pr:pr + 1]).then_inc(hi_ready, 1)

            def invert(done):
                act.wait_ge(den_made, done + 3)
                act.wait_ge(ctx_added, done + 1)
                nc.scalar.activation(part[:], den[:], ACT.Ln, bias=lo_sum).then_inc(ln_ready, 1)
                act.wait_ge(ln_ready, done + 2)
                nc.scalar.activation(part[:], part[:], ACT.Exp, scale=-1.0).then_inc(inverse_ready, 1)

            def cut_low(at, jt):
                slot = e[:, jt % EBUF, :, :]
                act.wait_ge(exp_ready, at + 1)
                nc.scalar.activation(slot, slot, ACT.Relu, bias=minus_lo).then_inc(cut, 1)

            def scale_v_sums(b):
                act.wait_ge(v_sum_ready, b + 1)
                for pr in range(PAIRS):
                    last = nc.scalar.activation(v_sum[:, pr, :], den[:, pr * NCH:(pr + 1) * NCH], ACT.Identity,
                                                bias=bv_lo[:, pr:pr + 1], scale=LO)
                last.then_inc(v_sum_made, 1)

            def attend(b, pr, nxt):
                t0, c0 = b * T_B + pr * T_PR, b * C_B + pr * C_PR

                def block_of(ib, first):
                    for jt in range(NT):
                        at = t0 + ib * T_IB + jt
                        act.wait_ge(scores_ready, at + 1)
                        act.wait_ge(p_used, at + (2 if jt % JC == 0 else 1))
                        if first and jt == 2:
                            act.wait_ge(k_stacked, (b * PAIRS + pr + 1) * S_K)
                        if first and jt == EBUF // 2:
                            act.wait_ge(q_stacked, (b * PAIRS + pr + 1) * S_Q)
                        nc.scalar.activation(e[:, jt % EBUF, :, :], sc[:, 2 * (jt % 2):2 * (jt % 2) + 2, :],
                                             ACT.Exp, scale=float(D) ** -0.5).then_inc(exp_ready, 1)
                        if not (first and jt == 0) and jt - 1 not in cuts_of(pr, ib):
                            cut_low(at - 1, (jt - 1) % NT)
                        if first and pr == 1:
                            if nxt:
                                make_h(jt)
                            make_o(jt)
                        if jt % JC == 0 and not (first and jt < LAG * JC):
                            invert(c0 + ib * C_IB + jt // JC - LAG)

                if pr == 1:
                    act.wait_ge(xr_in, 16 * b + 16)
                    act.wait_ge(kept, b + 1)
                    if nxt:
                        act.wait_ge(shift_ready, b + 2)
                block_of(0, True)
                with act.Fori(1, IB) as ib:
                    block_of(ib, False)
                cut_low(t0 + T_PR - 1, NT - 1)
                first, target = (g_qk1, g_qk_next)[pr](b), 1 - pr
                if pr == 0 or nxt:
                    act.wait_ge(p_used, EBUF + t0 + T_PR - 2 * JC)
                for c in range(LAG):
                    if pr == 0 or nxt:
                        high_halves(first, target, (2 * c, 2 * c + 1))
                    invert(c0 + C_PR - LAG + c)
                if pr == 0 or nxt:
                    high_halves(first, target, range(2 * LAG, G_QK))

            def batch(b, nxt):
                attend(b, 0, nxt)
                act.wait_ge(x1_stored, 16 * b + 16)
                attend(b, 1, nxt)
                if nxt:
                    scale_v_sums(b + 1)

            act.wait_ge(shift_ready, 1)
            for t in range(NT):
                make_h(t)
            act.wait_ge(weights_in, 176)
            high_halves(G_TR, 0, range(G_QK))
            act.wait_ge(const_ready, 4)
            act.wait_ge(bv_scaled, 1)
            scale_v_sums(0)
            act.wait_ge(mask_built, 2 * NT)
            with act.Fori(0, B - 1) as b:
                batch(b, True)
            batch(B - 1, False)

        @block.vector
        def _(dve):
            dve.sem_inc(group_free, 4)
            dve.sem_inc(chunk_free, 2)
            dve.sem_inc(ctx_added, 1)
            dve.sem_inc(behind_free, 1)

            def stats_of(src, t):
                nc.vector.bn_stats(stats[:, t, :], src[:, t, :]).then_inc(stats_made, 1)

            def aggregate(k):
                dve.wait_ge(stats_made, (k + 1) * NT)
                dve.sem_inc(waited, 1)
                for t in range(NT):
                    last = nc.vector.bn_aggr(mv[:, t, :], stats[:, t, :])
                last.then_inc(mv_ready, 1)

            def make_shift(k):
                dve.wait_ge(rstd_ready, k + 1)
                nc.vector.scalar_tensor_tensor(shift_x[:], mv[:, :, 0], -1.0, rstd_x[:], ALU.mult,
                                               ALU.mult).then_inc(shift_ready, 1)

            def keep():
                nc.vector.tensor_copy(rstd_r[:], rstd_x[:])
                nc.vector.tensor_copy(shift_r[:], shift_x[:]).then_inc(kept, 1)

            def move_hT(g):
                dve.wait_ge(group_ready, g + 1)
                nc.vector.tensor_copy(hT[:, g % KT, (g // KT) * IW:(g // KT + 1) * IW],
                                      sc[:, g % 4, :]).then_inc(group_free, 1)

            def low_half(first, g, pr, halves):
                hi, lo, bias = ((k_hi, k_lo, bk_c), (q_hi, q_lo, bq_c))[g // IB]
                cols = slice((g % IB) * IW, (g % IB + 1) * IW)
                dve.wait_ge(hi_ready, halves + g + 1)
                nc.vector.scalar_tensor_tensor(lo[:, cols], sc[:, g % 4, :], bias[:, pr:pr + 1],
                                               hi[:, cols], ALU.add, ALU.subtract).then_inc(group_free, 1)

            def move_v(first, g):
                dve.wait_ge(group_ready, first + g + 1)
                nc.vector.tensor_tensor(v[:, 2 * g:2 * g + 2, :], sc[:, g % 4, :].rearrange("p (a f) -> p a f", a=2),
                                        spread(bv_r[:], 2), ALU.add).then_inc(group_free, 1)

            def sum_h():
                nc.vector.reduce_sum(h_sum[:], hT[:].rearrange("p k (c n) -> p k c n", c=NCH),
                                     axis=AX_X).then_inc(h_summed, 1)

            def weigh(b, pr, at, ib, jt):
                slot = e[:, jt % EBUF, :, :]
                if jt in cuts_of(pr, ib):
                    dve.wait_ge(exp_ready, at + 1)
                    nc.vector.tensor_scalar(slot, slot, LO, 0.0, ALU.subtract, ALU.max).then_inc(cut_here, 1)
                    dve.wait_ge(cut_here, cuts(b, pr, ib, jt))
                else:
                    dve.wait_ge(cut, cuts_scalar(b, pr, ib, jt))
                nc.vector.scalar_tensor_tensor(slot, slot, HI - LO, spread(mask[:, jt, bass.ds(ib * IW, IW)], 2),
                                               ALU.min, ALU.mult).then_inc(p_ready, 1)

            def add_tiles(at, done, jt):
                dve.wait_ge(p_ready, at + 1)
                dve.wait_ge(den_made, done + 1)
                nc.vector.tensor_tensor(both[:, (jt // JC) % 2, :, :], e[:, (jt - 1) % EBUF, :, :], e[:, jt % EBUF, :, :],
                                        ALU.add).then_inc(both_ready, 1)

            def normalise(done, pr, c, cols, fresh):
                dve.wait_ge(p_used, EBUF + JC * (done + 1))
                dve.wait_ge(inverse_ready, done + 1)
                nc.vector.scalar_tensor_tensor(part[:], num[:, c % 2, :], v_sum[:, pr, c:c + 1],
                                               part[:], ALU.add, ALU.mult).then_inc(chunk_free, 1)
                dve.wait_ge(chunk_free, done + 3)
                if fresh:
                    nc.vector.tensor_copy(cols, part[:]).then_inc(ctx_added, 1)
                else:
                    nc.vector.tensor_tensor(cols, cols, part[:], ALU.add).then_inc(ctx_added, 1)

            def add_context(b, g, j):
                dve.wait_ge(behind_ready, j + 1)
                rows = o[:, 2 * g:2 * g + 2, :]
                nc.vector.tensor_tensor(rows, pj[:].rearrange("p (a f) -> p a f", a=2), rows,
                                        ALU.add).then_inc(behind_free, 1)

            def stats_of_o(g, j):
                dve.wait_ge(behind_free, j + 2)
                stats_of(o, 2 * g)
                stats_of(o, 2 * g + 1)

            def move_hT_group(g, j):
                dve.wait_ge(behind_ready, j + 1)
                nc.vector.tensor_copy(hT[:, g % KT, (g // KT) * IW:(g // KT + 1) * IW], pj[:]).then_inc(behind_free, 1)

            def centre(t):
                nc.vector.scalar_tensor_tensor(o[:, t, :], o[:, t, :], mv[:, t, 0:1], gamma_r[:], ALU.subtract,
                                               ALU.mult).then_inc(post_step, 1)

            def finish(b, t):
                dve.wait_ge(post_step, b * NT + t + 1)
                return nc.vector.scalar_tensor_tensor(o[:, t, :], o[:, t, :], rstd_o[:, t:t + 1], xr[:, t, :],
                                                      ALU.mult, ALU.add)

            def attend(b, pr, first_b, nxt):
                t0, c0 = b * T_B + pr * T_PR, b * C_B + pr * C_PR
                end_last = pr == 0 and not first_b

                def block_of(ib, first, last):
                    for jt in range(NT):
                        if jt % JC == 0 and not (first and jt < LAG * JC):
                            c = jt // JC - LAG
                            cols = ctxT[:, pr, bass.ds((ib if c >= 0 else ib - 1) * IW, IW)]
                            normalise(c0 + ib * C_IB + c, pr, c % NCH, cols, c == 0)
                        weigh(b, pr, t0 + ib * T_IB + jt, ib, jt)
                        if jt % JC == JC - 1 and jt // JC in adds_of(pr, ib):
                            add_tiles(t0 + ib * T_IB + jt, c0 + ib * C_IB + jt // JC, jt)
                        if first and end_last:
                            if jt == 0:
                                dve.wait_ge(bias_added, 2 * b)
                            if jt < G_WO:
                                add_context(b - 1, jt, j_wo(b) + jt)
                            if 1 <= jt <= G_WO:
                                stats_of_o(jt - 1, j_wo(b) + jt - 1)
                            if jt == G_WO + 1:
                                aggregate(2 * b)
                            if jt == G_WO + 2:
                                dve.wait_ge(mv_ready, 2 * b + 1)
                            if jt >= G_WO + 2:
                                for t in range(3 * (jt - G_WO - 2), min(3 * (jt - G_WO - 1), NT)):
                                    centre(t)
                        if last and end_last and jt < NT // 2:
                            if jt == 0:
                                dve.wait_ge(rstd_ready, 2 * b + 1)
                            finish(b - 1, 2 * jt)
                            done = finish(b - 1, 2 * jt + 1)
                            if jt == NT // 2 - 1:
                                done.then_inc(out_ready, 1)
                        if last and pr == 0 and nxt and jt >= NT // 2:
                            if jt == NT // 2:
                                dve.wait_ge(x_in, 16 * b + 16)
                            stats_of(h, 2 * jt - NT)
                            stats_of(h, 2 * jt - NT + 1)
                        if last and pr == 1 and nxt and jt < G_TR:
                            move_hT_group(jt, j_tr(b, first_b) + jt)

                block_of(0, True, False)
                with dve.Fori(1, IB - 1) as ib:
                    block_of(ib, False, False)
                block_of(IB - 1, False, True)
                if pr == 0 and nxt:
                    aggregate(2 * b + 1)
                for k in range(LAG):
                    if pr == 0 or nxt:
                        for g in (2 * k, 2 * k + 1):
                            low_half((g_qk1, g_qk_next)[pr](b), g, 1 - pr, (2 * b + 1 + pr) * G_QK)
                    c = NCH - LAG + k
                    normalise(c0 + C_PR - NCH + c, pr, c, ctxT[:, pr, N - IW:N], False)
                if pr == 0 and nxt:
                    make_shift(2 * b + 1)

            def batch(b, first, nxt):
                dve.wait_ge(v_sum_made, b + 1)
                attend(b, 0, first, nxt)
                for g in range(2 * LAG, G_QK):
                    low_half(g_qk1(b), g, 1, (2 * b + 1) * G_QK)
                attend(b, 1, first, nxt)
                nc.vector.drain().then_inc(ctx_done, 1)
                if nxt:
                    keep()
                    for g in range(2 * LAG, G_QK):
                        low_half(g_qk_next(b), g, 0, (2 * b + 2) * G_QK)
                    dve.wait_ge(behind_free, j_wo(b + 1) + 1)
                    sum_h()
                    for g in range(G_V):
                        move_v(g_v_next(b), g)
                else:
                    dve.wait_ge(bias_added, 2 * b + 2)
                    for g in range(G_WO):
                        add_context(b, g, j_wo(b + 1) - G_TR + g)
                        stats_of_o(g, j_wo(b + 1) - G_TR + g)
                    aggregate(2 * b + 1)
                    dve.wait_ge(mv_ready, 2 * b + 2)
                    for t in range(NT):
                        centre(t)
                    dve.wait_ge(rstd_ready, 2 * b + 2)
                    for t in range(NT):
                        last = finish(b, t)
                        if (t + 1) % (NT // X_IN) == 0:
                            last.then_inc(last_ready, 1)

            for t in range(NT):
                dve.wait_ge(x_begun[t * X_IN // NT], 16)
                stats_of(h, t)
            aggregate(0)
            make_shift(0)
            dve.wait_ge(shift_ready, 1)
            keep()
            for t in range(NT):
                dve.wait_ge(adj_in[t % STAGES], 16 * (t // STAGES + 1))
                nc.vector.tensor_scalar(mask[:, t, :], stage(t), 0.0, None, ALU.not_equal).then_inc(mask_built, 1)
                if t >= NEAR:
                    dve.wait_ge(near_stored[t % NEAR], 16)
                nc.vector.tensor_scalar(near_tile(t), stage(t), 0.0, None, ALU.is_gt).then_inc(mask_built, 1)
                if 2 <= t < 2 + G_TR // 2:
                    move_hT(2 * t - 4)
                    move_hT(2 * t - 3)
                if t == 2 + G_TR // 2:
                    dve.wait_ge(weights_in, 176)
                    nc.vector.tensor_scalar(bv_lo[:], bv_c[:], CHUNK * LO, None, ALU.mult).then_inc(bv_scaled, 1)
                    dve.wait_ge(group_free, G_TR + 4)
                    sum_h()
                if t >= NT - G_QK:
                    low_half(G_TR, t - (NT - G_QK), 0, 0)
            for k in range(NEAR):
                dve.wait_ge(near_stored[k], 32)
            for g in range(G_V):
                move_v(G_TR + G_QK, g)
            batch(0, True, True)
            with dve.Fori(1, B - 1) as b:
                batch(b, False, True)
            batch(B - 1, False, False)

        @block.tensor
        def _(pe):
            pe.wait_ge(const_ready, 4)
            pe.sem_inc(p_used, EBUF)
            pe.sem_inc(den_made, 2)

            def group(g):
                pe.wait_ge(group_free, g + 1)

            def transpose_h(first, tiles):
                for g in range(G_TR):
                    group(first + g)
                    pe.wait_ge(h_ready, tiles + 4 * (g // KT) + 4)
                    for k in range(4):
                        t = 4 * (g // KT) + k
                        last = nc.tensor.transpose(sc[:, g % 4, k * P:(k + 1) * P],
                                                   h[:, t, (g % KT) * P:(g % KT + 1) * P], ident[:])
                    last.then_inc(group_ready, 1)

            def project_qk(first, pr, groups):
                for g in groups:
                    group(first + g)
                    w = (wk, wq)[g // IB]
                    for kt in range(KT):
                        last = nc.tensor.matmul(sc[:, g % 4, :], w[:, kt, pr * P:(pr + 1) * P],
                                                hT[:, kt, (g % IB) * IW:(g % IB + 1) * IW],
                                                start=(kt == 0), stop=(kt == KT - 1))
                    last.then_inc(group_ready, 1)

            def project_v(first):
                for g in range(G_V):
                    group(first + g)
                    for k in range(2):
                        t = 2 * g + k
                        for kt in range(KT):
                            last = nc.tensor.matmul(sc[:, g % 4, k * F:(k + 1) * F], hT[:, kt, t * P:(t + 1) * P],
                                                    wv[:, kt, :], start=(kt == 0), stop=(kt == KT - 1))
                    last.then_inc(group_ready, 1)

            def project_context(g, j):
                pe.wait_ge(behind_free, j + 1)
                for k in range(2):
                    t = 2 * g + k
                    for pr in range(PAIRS):
                        last = nc.tensor.matmul(pj[:, k * F:(k + 1) * F], ctxT[:, pr, t * P:(t + 1) * P],
                                                wo[:, pr, :], start=(pr == 0), stop=(pr == PAIRS - 1))
                last.then_inc(behind_ready, 1)

            def transpose_next(g, j):
                pe.wait_ge(behind_free, j + 1)
                for k in range(4):
                    last = nc.tensor.transpose(pj[:, k * P:(k + 1) * P],
                                               h[:, 4 * (g // KT) + k, (g % KT) * P:(g % KT + 1) * P], ident[:])
                last.then_inc(behind_ready, 1)

            def score(ib, jt):
                rows = slice(jt * P, (jt + 1) * P)
                for hd in range(2):
                    out = sc[:, 2 * (jt % 2) + hd, :]
                    q = q_st[:, hd, bass.ds(ib * IW, IW)]
                    nc.tensor.matmul(out, kh_st[:, hd, rows], q, start=True, stop=False)
                    last = nc.tensor.matmul(out, kl_st[:, hd, rows], q, start=False, stop=True)
                last.then_inc(scores_ready, 1)

            def sum_v(b):
                pe.wait_ge(h_summed, b + 1)
                for pr in range(PAIRS):
                    for kt in range(KT):
                        last = nc.tensor.matmul(den[:, pr * NCH:(pr + 1) * NCH], wv[:, kt, pr * P:(pr + 1) * P],
                                                h_sum[:, kt, :], start=(kt == 0), stop=(kt == KT - 1))
                last.then_inc(v_sum_ready, 1)

            def apply(at, done, jt, pr, inc):
                c = (jt // JC) % 2
                if jt % JC == 0:
                    pe.wait_ge(chunk_free, done + 1)
                pe.wait_ge(p_ready, at + 1)
                for hd in range(2):
                    last = nc.tensor.matmul(num[hd * D:(hd + 1) * D, c, :],
                                            v[:, jt, pr * P + hd * D:pr * P + (hd + 1) * D],
                                            e[:, jt % EBUF, hd, :], start=(jt % JC == 0), stop=(jt % JC == JC - 1))
                if inc:
                    last.then_inc(p_used, inc)

            def sum_added(done, c, added):
                pe.wait_ge(both_ready, added)
                pe.wait_ge(ln_ready, done + 1)
                for hd in range(2):
                    last = nc.tensor.matmul(den[hd * D:(hd + 1) * D, :], ones[:], both[:, c % 2, hd, :],
                                            start=True, stop=True)
                last.then_inc(den_made, 1)

            def sum_tiles(at, done, jt):
                pe.wait_ge(p_ready, at + 1)
                pe.wait_ge(ln_ready, done + 1)
                for k in range(JC):
                    for hd in range(2):
                        last = nc.tensor.matmul(den[hd * D:(hd + 1) * D, :], ones[:],
                                                e[:, (jt - 1 + k) % EBUF, hd, :], start=(k == 0), stop=(k == JC - 1))
                last.then_inc(den_made, 1)

            def attend(b, pr, first_b, nxt, free_at):
                t0, c0 = b * T_B + pr * T_PR, b * C_B + pr * C_PR
                pe.wait_ge(k_begun, (b * PAIRS + pr + 1) * S_K)
                pe.wait_ge(q_begun, (b * PAIRS + pr + 1) * S_Q)
                for k in range(2):
                    pe.wait_ge(group_free, free_at + 2 * k - 2)
                    score(0, k)
                if pr == 0:
                    pe.wait_ge(v_sum_made, b + 1)

                def follow(ib, jt):
                    at, chunk = t0 + ib * T_IB + jt, c0 + ib * C_IB + jt // JC
                    c = (jt // JC) % NCH
                    added = jt < 0 or c in adds_of(pr, ib)
                    if jt % JC == JC - 1:
                        if added:
                            sum_added(chunk, c, adds(b, pr, ib, jt // JC))
                        else:
                            sum_tiles(at, chunk, jt % NT)
                    apply(at, chunk, jt % NT, pr, 1 if added else (2 if jt % JC == JC - 1 else 0))

                def block_of(ib, first, last):
                    for jt in range(NT):
                        if jt + 2 < NT or not last:
                            pe.wait_ge(exp_ready, t0 + ib * T_IB + jt + 1)
                            if first and jt + 2 == NT // 2:
                                pe.wait_ge(k_stacked, (b * PAIRS + pr + 1) * S_K)
                            if jt + 2 == NT:
                                pe.wait_ge(q_stacked, (b * PAIRS + pr + 1) * S_Q)
                            score(ib + (jt + 2) // NT, (jt + 2) % NT)
                        elif pr == 0 or nxt:
                            pe.wait_ge(exp_ready, t0 + ib * T_IB + jt + 1)
                            if pr and jt + 2 == NT:
                                pe.wait_ge(behind_free, j_wo(b + 1) + 1)
                            k = 2 * (jt + 2 - NT)
                            project_qk((g_qk1, g_qk_next)[pr](b), 1 - pr, (k, k + 1))
                        if not (first and jt < BEHIND):
                            follow(ib, jt - BEHIND)
                        if first and pr == 0 and not first_b and jt < G_WO:
                            project_context(jt, j_wo(b) + jt)
                        if last and pr == 1 and nxt and jt < G_TR:
                            if jt == 0:
                                pe.wait_ge(h_ready, (b + 2) * NT)
                            transpose_next(jt, j_tr(b, first_b) + jt)

                block_of(0, True, False)
                with pe.Fori(1, IB - 1) as ib:
                    block_of(ib, False, False)
                block_of(IB - 1, False, True)
                for k in range(BEHIND):
                    follow(IB, k - BEHIND)

            def batch(b, first, nxt):
                attend(b, 0, first, nxt, g_qk1(b) + 4)
                project_qk(g_qk1(b), 1, range(IB, G_QK))
                attend(b, 1, first, nxt, g_qk1(b) + G_QK + 4)
                if nxt:
                    project_qk(g_qk_next(b), 0, range(IB, G_QK))
                    project_v(g_v_next(b))
                    sum_v(b + 1)
                pe.wait_ge(ctx_done, b + 1)
                if not nxt:
                    for g in range(G_WO):
                        project_context(g, j_wo(b + 1) - G_TR + g)

            transpose_h(0, 0)
            pe.wait_ge(weights_in, 176)
            pe.wait_ge(group_free, G_TR + 4)
            project_qk(G_TR, 0, range(G_QK))
            project_v(G_TR + G_QK)
            sum_v(0)
            batch(0, True, True)
            with pe.Fori(1, B - 1) as b:
                batch(b, False, True)
            batch(B - 1, False, False)


def layer1(nc, x1, near, w, a, s_dram, out):
    B, N, F = x1.shape
    NT, KT, D = N // P, F // P, F // 4
    HEADS = F // D
    HW = 2 * IW
    FX = F + 2 * HEADS
    NH = KT * N // HW
    TB = NH * NT
    PB = 4
    TK = IW // P
    G_TR, G_PJ = KT * NT // 4, NT
    G_PREP = G_TR + G_PJ + 2
    G_END = 3
    X_IN = 4
    M_IN = 4
    ROWS, MEAN = G_PREP - 2, G_PREP - 1
    assert NH == 4 and KT == 2 and NT == 16

    behind = {t: [] for t in range(TB)}
    for n in range(NH):
        for k in range(G_END):
            behind[n * NT + 2 + k].append(("end", n - 1, k))
    for i, t in enumerate((31, 32, 33, 37)):
        behind[t] += [("prep", 2 * i), ("prep", 2 * i + 1)]
    for i in range(G_PJ // 2):
        behind[38 + i] += [("prep", G_TR + 2 * i), ("prep", G_TR + 2 * i + 1)]
    behind[49].append(("prep", ROWS))
    behind[53].append(("prep", MEAN))
    order = [g for t in range(TB) for g in behind[t]]

    with ExitStack() as ctx_:
        def sb(name, shape, dt):
            return ctx_.enter_context(nc.sbuf_tensor(name, shape, dt))

        def sem(name):
            return ctx_.enter_context(nc.semaphore(name))

        mask = sb("b_mask", [P, NT, N], U8)
        hv = sb("b_hv", [P, NT, F], F32)
        u = sb("b_u", [P, NT, F], F32)
        hT = sb("b_hT", [P, KT, N], F32)
        sd = sb("b_sd", [P, NT, 2 * HEADS], F32)
        g32 = sb("b_g32", [P, NT, HEADS, 32], F32)
        r = sb("b_r", [P, HEADS, N], F32)
        p = sb("b_p", [P, PB, 2, HW], F32)
        xr = sb("b_xr", [P, 2, 2 * TK, P], F32)
        num_s = sb("b_num_s", [P, 2, 2, IW], F32)
        den_s = sb("b_den_s", [P, 2, IW], F32)
        y = sb("b_y", [P, 2 * TK, P], F32)
        neg = sb("b_neg", [P, 2 * TK, P], F32)
        wx = sb("b_wx", [P, KT, FX], F32)
        a_r = sb("b_a", [P, 2 * D], F32)
        wa = sb("b_wa", [P, HEADS, D], F32)
        ident = sb("b_ident", [P, P], F32)
        ones = sb("b_ones", [P, P], F32)
        ones_h = sb("b_ones_h", [P, 1], F16)
        lone = sb("b_lone", [1, N], F32)
        lone_c = sb("b_lone_c", [P, NT], F32)
        mean_v, mean_next = sb("b_mean_v", [P, F], F32), sb("b_mean_next", [P, F], F32)
        s_c = sb("b_s_c", [P, HEADS, NT], F32)
        s_rows = sb("b_s_rows", [HEADS * NT, P], F32)
        g = sb("b_g", [P, HEADS, NT], F32)
        q, q_next = sb("b_q", [P, HEADS, NT], F32), sb("b_q_next", [P, HEADS, NT], F32)
        dmax = sb("b_dmax", [P, HEADS], F32)
        top = sb("b_top", [P, HEADS], F32)
        top_g, top_q = sb("b_top_g", [P, HEADS], F32), sb("b_top_q", [P, HEADS], F32)
        rz, den_c = sb("b_rz", [P, TK, 2, 2], F32), sb("b_den_c", [P, TK, 2, 2], F32)
        stats = sb("b_stats", [P, NT, 6], F32)
        mv = sb("b_mv", [P, NT, 2], F32)
        var_eps, half_neg = sb("b_var", [P, NT], F32), sb("b_half", [P, NT], F32)
        rstd, shift = sb("b_rstd", [P, NT], F32), sb("b_shift", [P, NT], F32)
        num = ctx_.enter_context(nc.psum_tensor("b_num", [P, 2, 2, IW], F32))
        den = ctx_.enter_context(nc.psum_tensor("b_den", [P, 2, IW], F32))
        pj = ctx_.enter_context(nc.psum_tensor("b_pj", [P, 2, IW], F32))

        weights_in = sem("b_weights_in")
        mask_in = [sem(f"b_mask_in{k}") for k in range(M_IN)]
        mask_built = sem("b_mask_built")
        mask_h_used = sem("b_mask_h_used")
        lone_ready = sem("b_lone_ready")
        lone_turned = sem("b_lone_turned")
        lone_kept = sem("b_lone_kept")
        den_ready = sem("b_den_ready")
        y_step = sem("b_y_step")
        mean_kept = sem("b_mean_kept")
        const_ready = sem("b_const_ready")
        pool_step = sem("b_pool_step")
        wa_step = sem("b_wa_step")
        wx_ready = sem("b_wx_ready")
        x_begun = [sem(f"b_x_begun{k}") for k in range(X_IN)]
        x_in = sem("b_x_in")
        xr_in = [sem("b_xr_in0"), sem("b_xr_in1")]
        out_stored = [sem("b_out_stored0"), sem("b_out_stored1")]
        stats_made = sem("b_stats_made")
        waited = sem("b_waited")
        mv_ready = sem("b_mv_ready")
        rstd_ready = sem("b_rstd_ready")
        shift_ready = sem("b_shift_ready")
        h_ready = sem("b_h_ready")
        prep_ready = sem("b_prep_ready")
        prep_free = sem("b_prep_free")
        s_c_ready = sem("b_s_c_ready")
        dmax_ready = sem("b_dmax_ready")
        top_ready = sem("b_top_ready")
        tops_scaled = sem("b_tops_scaled")
        gq_ready = sem("b_gq_ready")
        q_taken = sem("b_q_taken")
        u_ready = [sem("b_u_ready0"), sem("b_u_ready1")]
        s_out = sem("b_s_out")
        s_in = [sem(f"b_s_in{i}") for i in range(HEADS)]
        relu_r = sem("b_relu_r")
        r_ready = sem("b_r_ready")
        p_ready = sem("b_p_ready")
        p_used = sem("b_p_used")
        sums_copied = sem("b_sums_copied")
        end_ready = sem("b_end_ready")
        end_free = sem("b_end_free")
        neg_ready = sem("b_neg_ready")
        neg_exp = sem("b_neg_exp")
        elu_step = sem("b_elu_step")
        out_ready = sem("b_out_ready")

        block = ctx_.enter_context(nc.Block())

        def groups_of(first, nxt):
            return [g for g in order if (nxt or g[0] == "end") and not (first and g[:2] == ("end", -1))]

        def bank_of(first, nxt):
            begin = G_PREP if first else G_PREP + len(groups_of(True, True))
            assert len(groups_of(False, True)) % 2 == 0
            return {g: (begin + i) % 2 for i, g in enumerate(groups_of(first, nxt))}

        def last_banks():
            used = G_PREP + len(groups_of(True, True)) + len(groups_of(False, False))
            return [(used + k) % 2 for k in range(G_END)]

        def batches(eng, batch):
            batch(0, True, True)
            with eng.Fori(1, B - 1) as b:
                batch(b, False, True)
            batch(B - 1, False, False)

        def stage_h(t):
            return p[:, t % PB, 0, :].bitcast(F16)

        def rows_of(dram, b):
            return dram[bass.ds(b, 1), :, :].rearrange("a (t p) f -> p (a t) f", p=P)

        def part_of(dram, b, n):
            rows = dram[bass.ds(b, 1), (n % 2) * HW:(n % 2 + 1) * HW, (n // 2) * P:(n // 2 + 1) * P]
            return rows.rearrange("a (t p) f -> p (a t) f", p=P)

        @block.sync
        def _(sp):
            for k in range(X_IN):
                tiles = slice(k * NT // X_IN, (k + 1) * NT // X_IN)
                sp.dma_start(hv[:, tiles, :], rows_of(x1, 0)[:, tiles, :]).then_inc(x_begun[k], 16)
            sp.dma_start(wx[:, :, 0:F], w.rearrange("(k p) n -> p k n", p=P)).then_inc(weights_in, 16)
            sp.dma_start(a_r[:], a.rearrange("(a n) -> a n", a=1).broadcast_to([P, 2 * D])).then_inc(weights_in, 16)
            for k in range(M_IN):
                tiles = slice(k * NT // M_IN, (k + 1) * NT // M_IN)
                sp.dma_start(mask[:, tiles, :], near.rearrange("(t p) n -> p t n", p=P)[:, tiles, :]).then_inc(mask_in[k], 16)

            def rows_out(b):
                sp.wait_ge(prep_free, b * G_PREP + ROWS + 1)
                sp.sem_inc(waited, 1)
                sp.dma_start(s_dram, s_rows[:]).then_inc(s_out, 16)
                sp.wait_ge(s_out, 16 * b + 16)
                sp.sem_inc(waited, 1)

            def spread_s(b, heads):
                for hd in heads:
                    row = s_dram[hd * NT:(hd + 1) * NT, :].rearrange("(a t) p -> a (t p)", a=1)
                    sp.dma_start(r[:, hd, :], row.broadcast_to([P, N])).then_inc(s_in[hd], 16)

            def load_part(b, n, first):
                if not (first and n < 2):
                    sp.wait_ge(out_stored[n % 2], 16 * (2 * b + n // 2))
                    sp.sem_inc(waited, 1)
                sp.dma_start(xr[:, n % 2, :, :], part_of(x1, b, n)).then_inc(xr_in[n % 2], 16)

            def store_part(b, n):
                sp.wait_ge(out_ready, b * NH + n + 1)
                sp.sem_inc(waited, 1)
                sp.dma_start(part_of(out, b, n), xr[:, n % 2, :, :]).then_inc(out_stored[n % 2], 16)

            def batch(b, first, nxt):
                load_part(b, 0, first)
                if not first:
                    sp.wait_ge(p_ready, b * TB)
                    sp.sem_inc(waited, 1)
                spread_s(b, (2, 3))
                if nxt:
                    sp.wait_ge(u_ready[1], b + 1)
                    sp.sem_inc(waited, 1)
                    sp.dma_start(hv[:], rows_of(x1, b + 1)).then_inc(x_in, 16)
                if not first:
                    store_part(b - 1, 3)
                load_part(b, 1, first)
                store_part(b, 0)
                load_part(b, 2, first)
                store_part(b, 1)
                load_part(b, 3, first)
                if nxt:
                    for hd in (2, 3):
                        sp.wait_ge(s_in[hd], 16 * b + 16)
                        sp.sem_inc(waited, 1)
                    rows_out(b + 1)
                    sp.wait_ge(p_ready, b * TB + TB // 2)
                    sp.sem_inc(waited, 1)
                    spread_s(b + 1, (0, 1))
                store_part(b, 2)

            rows_out(0)
            spread_s(0, (0, 1))
            batches(sp, batch)
            store_part(B - 1, 3)
            for k in range(2):
                sp.wait_ge(out_stored[k], 16 * B * NH // 2)

        @block.gpsimd
        def _(pool):
            pool.memset(ident[:], 0.0).then_inc(pool_step, 1)
            pool.memset(half_neg[:], -0.5).then_inc(pool_step, 1)
            pool.memset(ones[:], 1.0).then_inc(const_ready, 1)
            pool.memset(ones_h[:], 1.0).then_inc(const_ready, 1)
            pool.wait_ge(pool_step, 2)
            pool.affine_select(out=ident[:], in_=ident[:], compare_op=ALU.not_equal, fill=1.0, base=0,
                               pattern=[[-1, P]], channel_multiplier=1).then_inc(const_ready, 1)
            with pool.Fori(0, B) as b:
                pool.wait_ge(mv_ready, b + 1)
                pool.sem_inc(waited, 1)
                nc.gpsimd.tensor_scalar(var_eps[:], mv[:, :, 1], EPS, None, ALU.add).then_inc(pool_step, 1)
                pool.wait_ge(pool_step, b + 3)
                nc.gpsimd.tensor_tensor(rstd[:], var_eps[:], half_neg[:], ALU.pow).then_inc(rstd_ready, 1)
                pool.wait_ge(dmax_ready, b + 1)
                pool.sem_inc(waited, 1)
                nc.gpsimd.partition_all_reduce(top[:], dmax[:], P, RMAX).then_inc(top_ready, 1)

        @block.scalar
        def _(act):
            nc.scalar.preload_act_table_set("natural_log_exp_and_others")

            def make_h(b):
                act.wait_ge(shift_ready, b + 1)
                for t in range(NT):
                    nc.scalar.activation(hv[:, t, :], hv[:, t, :], ACT.Relu, bias=shift[:, t:t + 1],
                                         scale=rstd[:, t:t + 1]).then_inc(h_ready, 1)

            def move_group(b, k, bank):
                act.wait_ge(prep_ready, b * G_PREP + k + 1)
                if k < G_TR:
                    nc.scalar.activation(hT[:, k % KT, (k // KT) * IW:(k // KT + 1) * IW], pj[:, bank, :],
                                         ACT.Copy).then_inc(prep_free, 1)
                elif k < G_TR + G_PJ:
                    nc.scalar.activation(hv[:, k - G_TR, :], pj[:, bank, 0:F], ACT.Copy)
                    nc.scalar.activation(sd[:, k - G_TR, :], pj[:, bank, F:FX], ACT.Copy).then_inc(prep_free, 1)
                elif k == ROWS:
                    nc.scalar.activation(s_rows[:], pj[0:HEADS * NT, bank, 0:P], ACT.Copy).then_inc(prep_free, 1)
                else:
                    nc.scalar.activation(mean_next[:], pj[:, bank, 0:F], ACT.Copy, scale=1.0 / N).then_inc(prep_free, 1)

            def make_gq(b):
                act.wait_ge(tops_scaled, b + 1)
                for hd in range(HEADS):
                    d = sd[:, :, HEADS + hd]
                    nc.scalar.activation(g[:, hd, :], d, ACT.Exp, bias=top_g[:, hd:hd + 1], scale=ALPHA)
                    last = nc.scalar.activation(q_next[:, hd, :], d, ACT.Exp, bias=top_q[:, hd:hd + 1],
                                                scale=1.0 - ALPHA)
                last.then_inc(gq_ready, 1)

            def make_r(b, heads):
                for hd in heads:
                    act.wait_ge(s_in[hd], 16 * b + 16)
                    nc.scalar.activation(r[:, hd, :], r[:, hd, :], ACT.Relu, bias=top[:, hd:hd + 1]).then_inc(relu_r, 1)
                    act.wait_ge(relu_r, b * HEADS + hd + 1)
                    nc.scalar.activation(r[:, hd, :], r[:, hd, :], ACT.Exp, scale=ALPHA - 1.0).then_inc(r_ready, 1)

            def copy_sums(b, n):
                act.wait_ge(p_used, PB + (b * NH + n + 1) * NT)
                nc.scalar.activation(den_s[:, n % 2, :], den[:, n % 2, :], ACT.Copy).then_inc(sums_copied, 1)
                nc.scalar.activation(num_s[:, n % 2, :, :], num[:, n % 2, :, :], ACT.Copy).then_inc(sums_copied, 1)

            def exp_neg(b, n):
                act.wait_ge(y_step, b * NH + n + 1)
                nc.scalar.activation(neg[:], y[:], ACT.Relu, scale=-1.0).then_inc(neg_ready, 1)
                act.wait_ge(neg_ready, b * NH + n + 1)
                nc.scalar.activation(neg[:], neg[:], ACT.Exp, scale=-1.0).then_inc(neg_exp, 1)

            def batch(b, first, nxt):
                at = bank_of(first, nxt)

                def move(k0, k1):
                    if nxt:
                        for k in range(k0, k1):
                            move_group(b + 1, k, at[("prep", k)])

                if not first:
                    copy_sums(b - 1, 3)
                make_r(b, (2, 3))
                if not first:
                    exp_neg(b - 1, 3)
                copy_sums(b, 0)
                exp_neg(b, 0)
                if nxt:
                    make_h(b + 1)
                copy_sums(b, 1)
                move(0, 6)
                exp_neg(b, 1)
                move(6, G_TR + G_PJ)
                copy_sums(b, 2)
                move(ROWS, ROWS + 1)
                if nxt:
                    make_gq(b + 1)
                    move(MEAN, MEAN + 1)
                exp_neg(b, 2)
                if nxt:
                    make_r(b + 1, (0, 1))

            make_h(0)
            for k in range(G_PREP):
                move_group(0, k, k % 2)
            make_gq(0)
            make_r(0, (0, 1))
            batches(act, batch)
            copy_sums(B - 1, 3)
            exp_neg(B - 1, 3)

        @block.vector
        def _(dve):
            def stats_of(t):
                nc.vector.bn_stats(stats[:, t, :], hv[:, t, :]).then_inc(stats_made, 1)

            def aggregate(b):
                dve.wait_ge(stats_made, (b + 1) * NT)
                dve.sem_inc(waited, 1)
                for t in range(NT):
                    last = nc.vector.bn_aggr(mv[:, t, :], stats[:, t, :])
                last.then_inc(mv_ready, 1)

            def make_shift(b):
                dve.wait_ge(rstd_ready, b + 1)
                nc.vector.scalar_tensor_tensor(shift[:], mv[:, :, 0], -1.0, rstd[:], ALU.mult,
                                               ALU.mult).then_inc(shift_ready, 1)

            def take_s(b):
                dve.wait_ge(prep_free, b * G_PREP + G_TR + G_PJ)
                nc.vector.tensor_copy(s_c[:].rearrange("p h t -> p t h"), sd[:, :, 0:HEADS]).then_inc(s_c_ready, 1)
                nc.vector.reduce_max(dmax[:], sd[:, :, HEADS:].rearrange("p t h -> p h t"),
                                     axis=AX_X).then_inc(dmax_ready, 1)

            def scale_top(b):
                dve.wait_ge(top_ready, b + 1)
                nc.vector.tensor_scalar(top_g[:], top[:], -ALPHA, None, ALU.mult)
                nc.vector.tensor_scalar(top_q[:], top[:], ALPHA - 1.0, None, ALU.mult).then_inc(tops_scaled, 1)

            def make_u(b, hd):
                dve.wait_ge(gq_ready, b + 1)
                cols = slice(hd * D, (hd + 1) * D)
                gain = g[:, hd, :].rearrange("p (t z) -> p t z", z=1)
                nc.vector.tensor_tensor(u[:, :, cols], hv[:, :, cols], gain.broadcast_to([P, NT, D]), ALU.mult)
                last = nc.vector.tensor_copy(g32[:, :, hd, :], gain.broadcast_to([P, NT, 32]))
                if hd % 2:
                    last.then_inc(u_ready[hd // 2], 1)

            def weigh(b, n, jt):
                dve.wait_ge(p_used, b * TB + n * NT + jt + 1)
                cols = slice((n % 2) * HW, (n % 2 + 1) * HW)
                for k in range(2):
                    hd = 2 * (n // 2) + k
                    last = nc.vector.scalar_tensor_tensor(p[:, jt % PB, k, :], r[:, hd, cols], q[:, hd, jt:jt + 1],
                                                          mask[:, jt, cols], ALU.max, ALU.mult)
                last.then_inc(p_ready, 1)

            def finish_sums(b, n, banks):
                m = b * NH + n
                if n == 0:
                    dve.wait_ge(mean_kept, b + 1)
                alone = lone_c[:, (n % 2) * 2 * TK:(n % 2 + 1) * 2 * TK]
                dve.wait_ge(end_ready, m * G_END + 1)
                sums = pj[:, banks[0], :].rearrange("p (k a i z) -> p k a i z", k=TK, a=2, i=2)[:, :, :, :, 0]
                nc.vector.tensor_tensor(den_c[:], sums, alone.rearrange("p (z i k) -> p k z i", z=1, i=2)
                                        .broadcast_to([P, TK, 2, 2]), ALU.add).then_inc(end_free, 1)
                dve.wait_ge(end_free, m * G_END + 1)
                nc.vector.reciprocal(rz[:], den_c[:]).then_inc(den_ready, 1)
                dve.wait_ge(den_ready, m + 1)
                for ib in range(2):
                    dve.wait_ge(end_ready, m * G_END + 2 + ib)
                    scale = rz[:, :, :, ib].rearrange("p k (a z) -> p k a z", z=1).broadcast_to([P, TK, 2, D])
                    nc.vector.tensor_tensor(y[:, ib * TK:(ib + 1) * TK, :].rearrange("p k (a d) -> p k a d", a=2),
                                            pj[:, banks[1 + ib], :].rearrange("p (k a d) -> p k a d", k=TK, a=2),
                                            scale, ALU.mult).then_inc(end_free, 1)
                dve.wait_ge(end_free, (m + 1) * G_END)
                for t in range(2 * TK):
                    last = nc.vector.scalar_tensor_tensor(y[:, t, :], mean_v[:, (n // 2) * P:(n // 2 + 1) * P],
                                                          alone[:, t:t + 1], y[:, t, :], ALU.mult, ALU.add)
                last.then_inc(y_step, 1)

            def finish_elu(b, n):
                m = b * NH + n
                dve.wait_ge(neg_exp, m + 1)
                nc.vector.scalar_tensor_tensor(y[:], y[:], 0.0, neg[:], ALU.max, ALU.add).then_inc(elu_step, 1)
                dve.wait_ge(xr_in[n % 2], 16 * (2 * b + n // 2) + 16)
                dve.wait_ge(elu_step, m + 1)
                part = xr[:, n % 2, :, :]
                nc.vector.scalar_tensor_tensor(part, y[:], -1.0, part, ALU.add, ALU.add).then_inc(out_ready, 1)

            def batch(b, first, nxt):
                at = bank_of(first, nxt)
                if not first:
                    dve.wait_ge(p_ready, b * TB)
                nc.vector.tensor_copy(q[:], q_next[:]).then_inc(q_taken, 1)
                dve.wait_ge(q_taken, b + 1)
                for n in range(NH):
                    if n % 2 == 0:
                        dve.wait_ge(r_ready, b * HEADS + n + 2)
                    for jt in range(NT):
                        weigh(b, n, jt)
                        i = n * NT + jt
                        if i in (4, 5):
                            make_u(b, i - 2)
                        if jt == 6 and not (first and n == 0):
                            bb, nn = (b, n - 1) if n else (b - 1, 3)
                            finish_sums(bb, nn, [at[("end", n - 1, k)] for k in range(G_END)])
                        if jt == 9 and not (first and n == 0):
                            finish_elu(*((b, n - 1) if n else (b - 1, 3)))
                        if i == 10:
                            dve.wait_ge(prep_free, (b + 1) * G_PREP)
                            nc.vector.tensor_copy(mean_v[:], mean_next[:]).then_inc(mean_kept, 1)
                        if nxt:
                            if 10 <= i < 10 + NT:
                                if i == 10:
                                    dve.wait_ge(x_in, 16 * b + 16)
                                stats_of(i - 10)
                            if i == 26:
                                aggregate(b + 1)
                            if i == 28:
                                make_shift(b + 1)
                            if i == 49:
                                take_s(b + 1)
                            if i == 50:
                                scale_top(b + 1)
                            if i in (52, 53):
                                make_u(b + 1, i - 52)

            for t in range(NT):
                dve.wait_ge(x_begun[t * X_IN // NT], 16)
                stats_of(t)
            aggregate(0)
            make_shift(0)
            dve.wait_ge(weights_in, 32)
            n = 0
            for kt in range(KT):
                for part in range(2):
                    if n:
                        dve.wait_ge(wa_step, 2 * n)
                    nc.vector.tensor_tensor(wa[:], wx[:, kt, 0:F].rearrange("p (h d) -> p h d", h=HEADS),
                                            spread(a_r[:, part * D:(part + 1) * D], HEADS), ALU.mult).then_inc(wa_step, 1)
                    dve.wait_ge(wa_step, 2 * n + 1)
                    nc.vector.reduce_sum(wx[:, kt, F + part * HEADS:F + (part + 1) * HEADS], wa[:],
                                         axis=AX_X).then_inc(wa_step, 1)
                    n += 1
            dve.wait_ge(wa_step, 2 * n)
            dve.sem_inc(wx_ready, 1)
            dve.wait_ge(const_ready, 2)
            for t in range(NT):
                dve.wait_ge(mask_in[t * M_IN // NT], 16)
                if t >= PB:
                    dve.wait_ge(mask_h_used, t - PB + 1)
                nc.vector.tensor_copy(stage_h(t), mask[:, t, :]).then_inc(mask_built, 1)
            dve.wait_ge(mask_h_used, NT)
            nc.vector.tensor_scalar(lone[:], num[0:1, :, :, :].rearrange("p a b n -> p (a b n)"), 0.0, None,
                                    ALU.is_equal).then_inc(lone_ready, 1)
            take_s(0)
            scale_top(0)
            dve.wait_ge(lone_turned, 1)
            nc.vector.tensor_copy(lone_c[:], num[:, 0, 0, 0:NT]).then_inc(lone_kept, 1)
            make_u(0, 0)
            make_u(0, 1)
            batches(dve, batch)
            finish_sums(B - 1, 3, last_banks())
            finish_elu(B - 1, 3)

        @block.tensor
        def _(pe):
            def prepare(b, k, bank):
                if k < G_TR:
                    pe.wait_ge(h_ready, b * NT + 4 * (k // KT) + 4)
                    for i in range(4):
                        t = 4 * (k // KT) + i
                        last = nc.tensor.transpose(pj[:, bank, i * P:(i + 1) * P],
                                                   hv[:, t, (k % KT) * P:(k % KT + 1) * P], ident[:])
                elif k < G_TR + G_PJ:
                    t = k - G_TR
                    if t == 0:
                        pe.wait_ge(prep_free, b * G_PREP + G_TR)
                    for kt in range(KT):
                        last = nc.tensor.matmul(pj[:, bank, 0:FX], hT[:, kt, t * P:(t + 1) * P], wx[:, kt, :],
                                                start=(kt == 0), stop=(kt == KT - 1))
                elif k == ROWS:
                    pe.wait_ge(s_c_ready, b + 1)
                    pe.sem_inc(waited, 1)
                    last = nc.tensor.transpose(pj[0:HEADS * NT, bank, 0:P], s_c[:].rearrange("p h t -> p (h t)"),
                                               ident[:])
                else:
                    for t in range(NT):
                        last = nc.tensor.matmul(pj[:, bank, 0:F], ones[:], hv[:, t, :],
                                                start=(t == 0), stop=(t == NT - 1))
                last.then_inc(prep_ready, 1)

            def finish(b, n, k, bank):
                pe.wait_ge(sums_copied, 2 * (b * NH + n) + min(k, 1) + 1)
                src = den_s[:, n % 2, :] if k == 0 else num_s[:, n % 2, k - 1, :]
                for i in range(TK):
                    last = nc.tensor.transpose(pj[:, bank, i * P:(i + 1) * P], src[:, i * P:(i + 1) * P], ident[:])
                last.then_inc(end_ready, 1)

            def released(b, group):
                if group[0] == "prep":
                    return prep_free, (b + 1) * G_PREP + group[1] + 1
                return end_free, (b * NH + group[1]) * G_END + group[2] + 1

            def batch(b, first, nxt):
                groups, at = groups_of(first, nxt), bank_of(first, nxt)
                if first:
                    before = [(prep_free, ROWS + 1), (prep_free, MEAN + 1)]
                else:
                    before = [released(b - 1, g_) for g_ in order[-2:]]
                frees = before + [released(b, g_) for g_ in groups]
                done = 0
                for n in range(NH):
                    s, pr = n % 2, n // 2
                    m = b * NH + n
                    if not (first and n < 2):
                        pe.wait_ge(sums_copied, 2 * (m - 1))
                    if n % 2 == 0:
                        pe.wait_ge(u_ready[pr], b + 1)
                    for jt in range(NT):
                        end = jt == NT - 1
                        pe.wait_ge(p_ready, b * TB + n * NT + jt + 1)
                        for ib in range(2):
                            for k in range(2):
                                nc.tensor.matmul(num[k * D:(k + 1) * D, s, ib, :],
                                                 u[:, jt, pr * P + k * D:pr * P + (k + 1) * D],
                                                 p[:, jt % PB, k, ib * IW:(ib + 1) * IW], start=(jt == 0), stop=end)
                        for ib in range(2):
                            for k in range(2):
                                c = 2 * k + ib
                                last = nc.tensor.matmul(den[c * 32:(c + 1) * 32, s, :], g32[:, jt, 2 * pr + k, :],
                                                        p[:, jt % PB, k, ib * IW:(ib + 1) * IW],
                                                        start=(jt == 0), stop=end)
                        last.then_inc(p_used, 1)
                        for g_ in behind[n * NT + jt]:
                            if g_ not in at:
                                continue
                            pe.wait_ge(*frees[done])
                            done += 1
                            if g_[0] == "prep":
                                prepare(b + 1, g_[1], at[g_])
                            else:
                                bb, nn = (b, g_[1]) if g_[1] >= 0 else (b - 1, 3)
                                finish(bb, nn, g_[2], at[g_])

            pe.wait_ge(const_ready, 3)
            for k in range(G_TR):
                if k >= 2:
                    pe.wait_ge(prep_free, k - 1)
                prepare(0, k, k % 2)
            for t in range(NT):
                pe.wait_ge(mask_built, t + 1)
                for k in range(N // IW):
                    last = nc.tensor.matmul(num[0:1, k // 2, k % 2, :], ones_h[:], stage_h(t)[:, k * IW:(k + 1) * IW],
                                            start=(t == 0), stop=(t == NT - 1))
                last.then_inc(mask_h_used, 1)
                if t == 0:
                    pe.wait_ge(wx_ready, 1)
                pe.wait_ge(prep_free, G_TR + t - 1)
                prepare(0, G_TR + t, (G_TR + t) % 2)
            for k in (ROWS, MEAN):
                pe.wait_ge(prep_free, k - 1)
                prepare(0, k, k % 2)
            pe.wait_ge(lone_ready, 1)
            for t in range(NT):
                last = nc.tensor.matmul(num[:, 0, 0, t:t + 1], lone[0:1, t * P:(t + 1) * P], ones[0:1, 0:1],
                                        start=True, stop=True)
            last.then_inc(lone_turned, 1)
            pe.wait_ge(lone_kept, 1)
            pe.sem_inc(p_used, PB)
            batches(pe, batch)
            for k in range(G_END):
                if k == 0:
                    pe.wait_ge(end_free, (B * NH - 1) * G_END)
                if k == 2:
                    pe.wait_ge(end_free, (B * NH - 1) * G_END + 1)
                finish(B - 1, 3, k, last_banks()[k])


def kernel(**inputs):
    import numpy as _np
    import concourse.bacc as _bacc
    from concourse import mybir as _mybir
    from concourse.bass_utils import run_bass_kernel_spmd as _run

    nc = _bacc.Bacc("TRN2", target_bir_lowering=False, num_devices=1)
    arrays = {}

    def put(name, a):
        a = _np.ascontiguousarray(a)
        arrays[name] = a
        return nc.dram_tensor(name, a.shape, _mybir.dt.from_np(a.dtype), kind="ExternalInput").ap()

    x = _np.asarray(inputs["x"])
    B, N, F = x.shape
    f32 = _mybir.dt.float32
    x_d = put("x", x)
    adjT = put("adjT", _np.asarray(inputs["adj"]).T)
    wT = {k: put(f"w{k}T", _np.asarray(inputs[f"L0_gnn_W{k}"]).T) for k in "qkvo"}
    bc = {k: put(f"b{k}_cols", _np.asarray(inputs[f"L0_gnn_b{k}"]).reshape(F // P, P).T) for k in "qkv"}
    br = {k: put(f"b{k}", inputs[f"L0_gnn_b{k}"]) for k in "vo"}
    gamma, beta = put("gamma", inputs["L0_gnn_gamma"]), put("beta", inputs["L0_gnn_beta"])
    w1, a1 = put("w1", inputs["L1_gnn_W"]), put("a1", inputs["L1_gnn_a"])
    x1 = nc.dram_tensor("x1", (B, N, F), f32, kind="Internal").ap()
    near = nc.dram_tensor("near", (N, N), _mybir.dt.uint8, kind="Internal").ap()
    s_rows = nc.dram_tensor("s_rows", (4 * N // P, P), f32, kind="Internal").ap()
    out = nc.dram_tensor("out", (B, N, F), f32, kind="ExternalOutput").ap()
    layer0(nc, x_d, adjT, wT["q"], bc["q"], wT["k"], bc["k"], wT["v"], br["v"], bc["v"], wT["o"], br["o"], gamma, beta, near, x1)
    layer1(nc, x1, near, w1, a1, s_rows, out)
    r = _run(nc, [arrays], core_ids=[0])
    return r.results[0]["out"]
```
